# Optimizing a Trainium2 kernel written in Bass

```python
import numpy as np
import jax
import jax.numpy as jnp

def _softmax(x, axis=-1):
    return jax.nn.softmax(x, axis=axis)

def _gelu(x):
    return jax.nn.gelu(x, approximate=True)

def _silu(x):
    return jax.nn.silu(x)

def _sigmoid(x):
    return jax.nn.sigmoid(x)

def _layernorm(x, axis=-1, eps=1e-05):
    m = jnp.mean(x, axis=axis, keepdims=True)
    v = jnp.var(x, axis=axis, keepdims=True)
    return (x - m) / jnp.sqrt(v + eps)

def _scatter_add(tgt, idx, src, axis=0):
    return tgt.at[idx].add(src)

def _segment_sum(src, seg, n):
    return jax.ops.segment_sum(src, seg, n)
kernel_name = 'mk_gnn_preln_d2_gnn_r8_1a0f18'

def setup_inputs(seed: int=0):
    np.random.seed(seed)
    _w = jnp.asarray

    def _rec_inputs():
        import jax
        import jax.numpy as jnp
        _gk = jax.random.key(seed)
        x = -0.0008691 + 1 * jax.random.normal(jax.random.fold_in(_gk, 1), (12500, 128), jnp.float32)
        _s = jax.random.randint(jax.random.fold_in(_gk, 2), (100000,), 0, 12500, jnp.int32)
        _d = jax.random.randint(jax.random.fold_in(_gk, 3), (100000,), 0, 12500, jnp.int32)
        _loop = jnp.arange(12500, dtype=jnp.int32)
        src = jnp.concatenate([_s, _d, _loop])
        dst = jnp.concatenate([_d, _s, _loop])
        _o = jnp.argsort(dst, stable=True)
        src = src[_o]
        dst = dst[_o]
        edge_type_2 = jax.random.randint(jax.random.fold_in(_gk, 12), (212500,), 0, 2, jnp.int32)
        return (x, src, dst, edge_type_2)
    x, src, dst, edge_type_2 = _rec_inputs()

    def _L0_gnn_setup():
        import jax, jax.numpy as jnp
        import numpy as np
        IN_DIM = 128
        OUT_DIM = 128
        N_NODES = 1250
        N_EDGES = 80000
        key = jax.random.key(seed)
        ks = jax.random.split(key, 9)
        X = jax.random.normal(ks[0], (N_NODES, IN_DIM), dtype=jnp.float32)
        edge_index = jax.random.randint(ks[1], (2, N_EDGES), 0, N_NODES, dtype=jnp.int64)
        edge_types = jax.random.randint(ks[2], (N_EDGES,), 0, 2, dtype=jnp.int64)
        s = 1.0 / np.sqrt(IN_DIM)
        W_data = jax.random.uniform(ks[3], (OUT_DIM, IN_DIM), minval=-s, maxval=s, dtype=jnp.float32)
        b_data = jax.random.uniform(ks[4], (OUT_DIM,), minval=-s, maxval=s, dtype=jnp.float32)
        W_control = jax.random.uniform(ks[5], (OUT_DIM, IN_DIM), minval=-s, maxval=s, dtype=jnp.float32)
        b_control = jax.random.uniform(ks[6], (OUT_DIM,), minval=-s, maxval=s, dtype=jnp.float32)
        W_self = jax.random.uniform(ks[7], (OUT_DIM, IN_DIM), minval=-s, maxval=s, dtype=jnp.float32)
        b_self = jax.random.uniform(ks[8], (OUT_DIM,), minval=-s, maxval=s, dtype=jnp.float32)
        return {'X': X, 'edge_index': edge_index, 'edge_types': edge_types, 'W_data': W_data, 'b_data': b_data, 'W_control': W_control, 'b_control': b_control, 'W_self': W_self, 'b_self': b_self}
    _L0_gnn_all = _L0_gnn_setup()
    _L0_gnn_in = {k: v for k, v in _L0_gnn_all.items() if k in ('W_data', 'b_data', 'W_control', 'b_control', 'W_self', 'b_self')}
    del _L0_gnn_all

    def _L1_gnn_setup():
        import jax, jax.numpy as jnp
        import numpy as np
        N = 6250
        E = 80000
        D = 128
        NUM_LAYERS = 2
        key = jax.random.key(seed)
        k1, k2 = jax.random.split(key)
        emb = jax.random.normal(k1, (N, D), dtype=jnp.float32)
        edge_index = jax.random.randint(k2, (2, E), 0, N, dtype=jnp.int64)
        return {'emb': emb, 'edge_index': edge_index}
    _L1_gnn_all = _L1_gnn_setup()
    _L1_gnn_in = {k: v for k, v in _L1_gnn_all.items() if k in ()}
    del _L1_gnn_all
    return {'x': x, 'src': src, 'dst': dst, 'edge_type_2': edge_type_2, 'L0_gnn_W_data': _L0_gnn_in['W_data'], 'L0_gnn_b_data': _L0_gnn_in['b_data'], 'L0_gnn_W_control': _L0_gnn_in['W_control'], 'L0_gnn_b_control': _L0_gnn_in['b_control'], 'L0_gnn_W_self': _L0_gnn_in['W_self'], 'L0_gnn_b_self': _L0_gnn_in['b_self']}

def reference(x, src, dst, edge_type_2, L0_gnn_W_data, L0_gnn_b_data, L0_gnn_W_control, L0_gnn_b_control, L0_gnn_W_self, L0_gnn_b_self):
    import jax
    import jax.numpy as jnp

    def _L0_gnn_ref(X, edge_index, edge_types, W_data, b_data, W_control, b_control, W_self, b_self):
        import jax, jax.numpy as jnp
        import numpy as np
        IN_DIM = 128
        OUT_DIM = 128
        N_NODES = 1250
        N_EDGES = 80000
        src, dst = (edge_index[0], edge_index[1])
        Xs = X[src]
        m_data = Xs @ W_data.T + b_data
        m_ctrl = Xs @ W_control.T + b_control
        msg = jnp.where((edge_types == 0)[:, None], m_data, m_ctrl)
        agg = jax.ops.segment_sum(msg, dst, num_segments=X.shape[0])
        out = agg + (X @ W_self.T + b_self)
        return jax.nn.relu(out)

    def _L1_gnn_ref(emb, edge_index):
        import jax, jax.numpy as jnp
        import numpy as np
        N = 6250
        E = 80000
        D = 128
        NUM_LAYERS = 2
        row, col = (edge_index[0], edge_index[1])
        n = emb.shape[0]
        ones = jnp.ones(row.shape[0], dtype=emb.dtype)
        deg = jax.ops.segment_sum(ones, col, num_segments=n)
        deg_inv_sqrt = jnp.where(deg > 0, jax.lax.rsqrt(deg), 0.0).astype(emb.dtype)
        norm = deg_inv_sqrt[row] * deg_inv_sqrt[col]
        x = emb
        out = x
        for _ in range(NUM_LAYERS):
            msgs = x[row] * norm[:, None]
            x = jax.ops.segment_sum(msgs, col, num_segments=n)
            out = out + x
        return out / (NUM_LAYERS + 1)
    edge_index = jnp.stack([src, dst])
    h = jnp.maximum(_layernorm(x, axis=-1), 0.0)
    x = x + _L0_gnn_ref(h, edge_index, edge_type_2, L0_gnn_W_data, L0_gnn_b_data, L0_gnn_W_control, L0_gnn_b_control, L0_gnn_W_self, L0_gnn_b_self)
    h = jnp.maximum(_layernorm(x, axis=-1), 0.0)
    x = x + _L1_gnn_ref(h, edge_index)
    return x

_drawn_inputs = setup_inputs


def setup_inputs(seed=0):
    import zlib

    import numpy as np

    out = dict(_drawn_inputs(seed))
    spreads = {}
    factors = {'L0_gnn_b_self': 3.353}
    for name, (base, spread) in spreads.items():
        noise = np.random.default_rng([zlib.crc32(name.encode()), seed]).standard_normal(out[name].shape)
        drawn = base * np.exp(spread * noise) if base else spread * noise
        out[name] = jnp.asarray(drawn.astype(out[name].dtype))
    for name, factor in factors.items():
        out[name] = (out[name] * factor).astype(out[name].dtype)
    return out
```

```python
from contextlib import ExitStack

import concourse.bass as bass
from concourse import mybir

P = 128
CHUNKS = 8
GROUP = CHUNKS * P
TILE_GROUPS = P // CHUNKS
SLOTS = 4
PAIR = 2
FIVE = 5
FAR = 1 << 20
EPS = 1e-5
HOPS = 2

F32 = mybir.dt.float32
BF16 = mybir.dt.bfloat16
I32 = mybir.dt.int32
ALU = mybir.AluOpType
ACT = mybir.ActivationFunctionType
AX_X = mybir.AxisListType.X
ds = bass.ds


class Steps:

    def __init__(self, engine, semaphore):
        self.engine, self.semaphore, self.done = engine, semaphore, 0
        self.turn = self.per = 0

    def enter(self, turn, per):
        self.turn, self.per, self.first = turn, per, self.done

    def leave(self, times):
        assert self.done - self.first == self.per
        self.done = self.first + self.per * times
        self.turn = self.per = 0

    def then_wait(self, instruction, also=None):
        instruction.then_inc(self.semaphore, 1)
        self.done += 1
        value = self.turn * self.per + self.done
        if also:
            self.engine.compute_val(value)
            self.engine.wait_ge(*also)
        self.engine.wait_ge(self.semaphore, value)


def ready_early(engine, *values):
    for value in values:
        engine.compute_val(value)
    return values


def gnn_kernel(nc, x, src, dst, edge_type, w_data, b_data, w_control, b_control, w_self, b_self, out):
    n_nodes, features = x.shape
    n_edges = src.shape[0]
    assert features == P

    batch = FIVE * P
    padded = -(-n_nodes // (2 * batch)) * 2 * batch
    while padded % (2 * PAIR * P):
        padded += 2 * batch
    blocks = padded // P
    whole = n_nodes // P
    tail = n_nodes - whole * P
    pair_turns = blocks // (2 * PAIR)
    five_turns = blocks // (2 * FIVE)
    assert padded - n_nodes < 2 * batch and blocks <= P

    tiles = -(-n_edges // (P * P))
    chunks = tiles * P
    groups = tiles * TILE_GROUPS
    turns = groups // SLOTS
    last_edge = (tiles - 1) * P * P
    full_rows = (n_edges - last_edge) // P
    odd_edges = n_edges - last_edge - full_rows * P

    table = nc.dram_tensor("table", (2 * padded, P), F32, kind="Internal").ap()
    base_dram = nc.dram_tensor("base_dram", (1, groups), I32, kind="Internal").ap()

    with ExitStack() as ctx:
        def sbuf(name, shape, dtype=F32):
            return ctx.enter_context(nc.sbuf_tensor(name, [P, *shape], dtype))

        def semaphore(name):
            return ctx.enter_context(nc.semaphore(name))

        state = sbuf("state", [padded])
        acc = sbuf("acc", [padded + P])
        index_typed = sbuf("index_typed", [chunks], I32)
        index_plain = sbuf("index_plain", [chunks], I32)
        local = sbuf("local", [chunks])
        rest = sbuf("rest", [chunks])
        dst_block = sbuf("dst_block", [chunks], I32)
        dst_row = sbuf("dst_row", [chunks], I32)
        raw_dst = sbuf("raw_dst", [tiles, P], I32)
        rows = sbuf("rows", [SLOTS, CHUNKS, P])
        hot = sbuf("hot", [SLOTS, CHUNKS, P])
        ring_index = sbuf("ring_index", [SLOTS, CHUNKS], I32)
        hot_row = sbuf("hot_row", [2, CHUNKS, P], BF16)
        hot_block = sbuf("hot_block", [2, CHUNKS, blocks], BF16)
        zeros = sbuf("zeros", [batch])
        iota = sbuf("iota", [P], I32)
        identity = sbuf("identity", [P])
        weights = sbuf("weights", [3, P])
        w_types = sbuf("w_types", [2 * P])
        w_own = sbuf("w_own", [P])
        b_types = sbuf("b_types", [2 * P])
        b_own = sbuf("b_own", [1])
        bn = sbuf("bn", [2 * FIVE, 6])
        moments = sbuf("moments", [2 * FIVE, 2])
        stats = sbuf("stats", [blocks, 2])
        spread = sbuf("spread", [blocks])
        rstd = sbuf("rstd", [blocks])
        shift = sbuf("shift", [blocks])
        inv = sbuf("inv", [blocks])
        inv_third = sbuf("inv_third", [blocks])
        linked = sbuf("linked", [blocks])
        chunk_min = sbuf("chunk_min", [tiles])
        group_min = sbuf("group_min", [TILE_GROUPS])
        group_base = sbuf("group_base", [TILE_GROUPS], I32)
        base_row = sbuf("base_row", [groups], I32)
        base_all = sbuf("base_all", [groups], I32)
        rest_min = sbuf("rest_min", [1])
        any_rest = sbuf("any_rest", [1])
        rest_flag = sbuf("rest_flag", [1], I32)
        window = sbuf("window", [CHUNKS])

        raw_src = hot[:, 0:2].rearrange("p s c f -> p (s c f)")[:, 0:chunks].bitcast(I32)
        raw_type = hot[:, 2:4].rearrange("p s c f -> p (s c f)")[:, 0:chunks].bitcast(I32)
        flat = rows[:, :].rearrange("p s c f -> p (s c f)")

        def carve(start, size):
            return [flat[:, start + i * size:start + (i + 1) * size] for i in range(2)]

        normed = carve(0, PAIR * P)
        normed_t = carve(2 * PAIR * P, PAIR * P)
        messages = carve(4 * PAIR * P, 2 * PAIR * P)
        staged = carve(0, batch)
        fresh = carve(2 * batch, batch)
        scaled = carve(4 * batch, batch)
        assert 6 * batch <= SLOTS * GROUP and chunks <= 2 * GROUP

        banks = ctx.enter_context(nc.psum_tensor("banks", [P, 4, 512], F32))
        degree = ctx.enter_context(nc.psum_tensor("degree", [P, 512], F32))[:, 0:blocks]
        count_up = ctx.enter_context(nc.psum_tensor("count_up", [P, 512], F32))[:, 0:P]
        typed_banks = ctx.enter_context(nc.psum_tensor("typed_banks", [P, 2, 512], F32))
        turned = [banks[:, 2 * i:2 * i + 2].rearrange("p a f -> p (a f)")[:, 0:batch] for i in range(2)]

        edges_in = semaphore("edges_in")
        weights_in = semaphore("weights_in")
        x_in = semaphore("x_in")
        padded_edges = semaphore("padded_edges")
        padded_x = semaphore("padded_x")
        zeroed = semaphore("zeroed")
        iota_made = semaphore("iota_made")
        identity_made = semaphore("identity_made")
        weights_turned = semaphore("weights_turned")
        weights_copied = semaphore("weights_copied")
        edges_ready = semaphore("edges_ready")
        tile_turned = semaphore("tile_turned")
        tile_copied = semaphore("tile_copied")
        min_ready = semaphore("min_ready")
        min_turned = semaphore("min_turned")
        base_made = semaphore("base_made")
        base_stored = semaphore("base_stored")
        base_in = semaphore("base_in")
        rest_ready = semaphore("rest_ready")
        rest_turned = semaphore("rest_turned")
        prepared = semaphore("prepared")
        variance_ready = semaphore("variance_ready")
        spread_ready = semaphore("spread_ready")
        norm_ready = semaphore("norm_ready")
        h_ready = [semaphore(f"h_ready{i}") for i in range(2)]
        h_turned = [semaphore(f"h_turned{i}") for i in range(2)]
        h_copied = [semaphore(f"h_copied{i}") for i in range(2)]
        typed_summed = [semaphore(f"typed_summed{i}") for i in range(2)]
        own_summed = [semaphore(f"own_summed{i}") for i in range(2)]
        own_copied = [semaphore(f"own_copied{i}") for i in range(2)]
        message_ready = [semaphore(f"message_ready{i}") for i in range(2)]
        message_stored = [semaphore(f"message_stored{i}") for i in range(2)]
        index_ready = [semaphore(f"index_ready{j}") for j in range(SLOTS)]
        rows_landed = [semaphore(f"rows_landed{j}") for j in range(SLOTS)]
        hot_ready = [semaphore(f"hot_ready{j}") for j in range(SLOTS)]
        summed = [semaphore(f"summed{j}") for j in range(SLOTS)]
        added = [semaphore(f"added{j}") for j in range(SLOTS)]
        degree_hot = [semaphore(f"degree_hot{i}") for i in range(2)]
        degree_summed = [semaphore(f"degree_summed{i}") for i in range(2)]
        rest_index = semaphore("rest_index")
        rest_landed = semaphore("rest_landed")
        rest_hot = semaphore("rest_hot")
        rest_summed = semaphore("rest_summed")
        rest_added = semaphore("rest_added")
        rest_step = semaphore("rest_step")
        pass_done = semaphore("pass_done")
        degree_bounded = semaphore("degree_bounded")
        degree_root = semaphore("degree_root")
        stage_ready = [semaphore(f"stage_ready{i}") for i in range(2)]
        stage_turned = [semaphore(f"stage_turned{i}") for i in range(2)]
        turned_used = [semaphore(f"turned_used{i}") for i in range(2)]
        acc_cleared = semaphore("acc_cleared")
        fresh_ready = [semaphore(f"fresh_ready{i}") for i in range(2)]
        fresh_used = [semaphore(f"fresh_used{i}") for i in range(2)]
        scaled_ready = [semaphore(f"scaled_ready{i}") for i in range(2)]
        scaled_stored = [semaphore(f"scaled_stored{i}") for i in range(2)]
        step = semaphore("step")

        rest_turns = groups * blocks

        def blocks_of(ap, n):
            return ap.rearrange("p (b f) -> p b f", b=n)

        def over_features(ap, n):
            return ap.unsqueeze(2).to_broadcast([P, n, P])

        def over_hot(ap, columns):
            return ap.unsqueeze(2).to_broadcast([P, CHUNKS, columns])

        def counting(columns):
            return count_up[:, 0:columns].unsqueeze(1).to_broadcast([P, CHUNKS, columns])

        def table_rows(first, n):
            return table[ds(first, n * P), :].rearrange("(b p) f -> p b f", p=P)

        block = ctx.enter_context(nc.Block())

        @block.sync
        def _(sp):
            sp.wait_ge(padded_edges, 3)
            for raw, array in ((raw_src, src), (raw_type, edge_type), (raw_dst[:, :].rearrange("p k e -> p (k e)"), dst)):
                by_tile = raw.rearrange("p (k e) -> p k e", k=tiles)
                if tiles > 1:
                    sp.dma_start(by_tile[:, 0:tiles - 1, :],
                                 array[0:last_edge].rearrange("(k p e) -> p k e", p=P, e=P)).then_inc(edges_in, 16)
                if full_rows:
                    sp.dma_start(by_tile[0:full_rows, tiles - 1, :],
                                 array[last_edge:last_edge + full_rows * P].rearrange("(p e) -> p e", e=P)
                                 ).then_inc(edges_in, 16)
                if odd_edges:
                    sp.dma_start(by_tile[full_rows:full_rows + 1, tiles - 1, 0:odd_edges],
                                 array[n_edges - odd_edges:n_edges].rearrange("(p e) -> p e", p=1)
                                 ).then_inc(edges_in, 16)
            sp.wait_ge(base_made, 1)
            sp.dma_start(base_dram.rearrange("a (k g) -> (a k) g", k=tiles), group_base[0:tiles, :]).then_inc(base_stored, 16)
            sp.wait_ge(base_stored, 16)
            sp.dma_start(base_row[0:1, :], base_dram).then_inc(base_in, 16)
            sp.dma_start(base_all[:, :], base_dram[0, :].partition_broadcast(P)).then_inc(base_in, 16)
            with sp.Fori(0, pair_turns) as t:
                for i in range(2):
                    first = (t * 2 + i) * (PAIR * P)
                    sp.wait_ge(message_ready[i], t + 1)
                    by_type = messages[i].rearrange("p (b k f) -> p b k f", b=PAIR, k=2)
                    for k in range(2):
                        sp.dma_start(table_rows(first + k * padded, PAIR), by_type[:, :, k, :]).then_inc(message_stored[i], 16)
            for hop in range(HOPS):
                with sp.Fori(0, five_turns) as t:
                    for i in range(2):
                        sp.wait_ge(scaled_ready[i], t + (hop * five_turns + 1))
                        sp.dma_start(table_rows((t * 2 + i) * batch, FIVE), blocks_of(scaled[i], FIVE)).then_inc(scaled_stored[i], 16)
            stores = (HOPS * five_turns + 1)
            with sp.Fori(0, five_turns - 1) as t:
                for i in range(2):
                    sp.wait_ge(scaled_ready[i], t + stores)
                    sp.dma_start(out[ds((t * 2 + i) * batch, batch), :].rearrange("(b p) f -> p b f", p=P),
                                 blocks_of(scaled[i], FIVE)).then_inc(scaled_stored[i], 16)
            parts = [0, 0]
            for i in range(2):
                first = ((five_turns - 1) * 2 + i) * FIVE
                sp.wait_ge(scaled_ready[i], (HOPS + 1) * five_turns)
                n = max(0, min(FIVE, whole - first))
                if n:
                    sp.dma_start(out[first * P:(first + n) * P, :].rearrange("(b p) f -> p b f", p=P),
                                 blocks_of(scaled[i], FIVE)[:, 0:n, :]).then_inc(scaled_stored[i], 16)
                    parts[i] += 1
                if tail and 0 <= whole - first < FIVE:
                    sp.dma_start(out[whole * P:n_nodes, :], blocks_of(scaled[i], FIVE)[0:tail, whole - first, :]
                                 ).then_inc(scaled_stored[i], 16)
                    parts[i] += 1
            for i in range(2):
                sp.wait_ge(scaled_stored[i], 16 * ((HOPS + 1) * five_turns - 1 + parts[i]))

        @block.gpsimd
        def _(pool):
            pool.memset(zeros[:, :], 0.0).then_inc(zeroed, 1)
            pool.memset(identity[:, :], 0.0).then_inc(zeroed, 1)
            pool.iota(iota[:, :], pattern=[[1, P]], base=0, channel_multiplier=0).then_inc(iota_made, 1)
            pool.wait_ge(zeroed, 2)
            pool.affine_select(out=identity[:, :], in_=identity[:, :], compare_op=ALU.not_equal, fill=1.0,
                               base=0, pattern=[[-1, P]], channel_multiplier=1).then_inc(identity_made, 1)

            def gather(index, into, landed, slot):
                for c in range(CHUNKS):
                    pool.indirect_dma_start(
                        out=into[:, slot, c, :], out_offset=None, in_=table,
                        in_offset=bass.IndirectOffsetOnAxis(ap=index[:, slot, c:c + 1], axis=0)).then_inc(landed, 16)

            def clear_sums(passes):
                with pool.Fori(0, five_turns) as t:
                    for i in range(2):
                        pool.wait_ge(stage_ready[i], t + ((passes - 1) * five_turns + 1))
                        pool.tensor_copy(acc[:, ds((t * 2 + i) * batch, batch)], zeros[:, :]).then_inc(acc_cleared, 1)

            for k in range(1 + HOPS):
                if k:
                    clear_sums(k)
                stored = [(message_stored[i], 32 * pair_turns) if k == 0 else (scaled_stored[i], 16 * k * five_turns)
                          for i in range(2)]
                pool.wait_ge(*stored[0])
                pool.wait_ge(fresh_used[0], k * five_turns)
                pool.wait_ge(fresh_used[1], k * five_turns)
                with pool.Fori(0, turns) as t:
                    for j in range(SLOTS):
                        uses, before = ready_early(pool, t + (k * turns + 1), t + k * turns)
                        pool.wait_ge(*stored[1])
                        pool.wait_ge(index_ready[j], uses)
                        pool.wait_ge(summed[j], before)
                        gather(ring_index, rows, rows_landed[j], j)
                if k == 0:
                    pool.wait_ge(prepared, 1)
                flag = pool.value_load(rest_flag[0:1, 0:1], min_val=0, max_val=1)
                with pool.If(flag > 0):
                    pool.wait_ge(summed[0], (k + 1) * turns)
                    with pool.Fori(0, groups) as g:
                        uses, before = ready_early(pool, g + (k * groups + 1), g * blocks + k * rest_turns)
                        pool.wait_ge(*stored[1])
                        pool.wait_ge(rest_index, uses)
                        pool.wait_ge(rest_summed, before)
                        gather(ring_index, rows, rest_landed, 0)
                    pool.nop()

        @block.scalar
        def _(act):
            for n, w in enumerate((w_data, w_control, w_self)):
                act.dma_start(weights[:, n, :], w).then_inc(weights_in, 16)
            act.dma_start(b_types[:, 0:P], b_data.partition_broadcast(P)).then_inc(weights_in, 16)
            act.dma_start(b_types[:, P:2 * P], b_control.partition_broadcast(P)).then_inc(weights_in, 16)
            act.dma_start(b_own[:, :], b_self.rearrange("(p a) -> p a", a=1)).then_inc(weights_in, 16)
            act.wait_ge(padded_x, 1)
            if whole:
                act.dma_start(blocks_of(state[:, 0:whole * P], whole),
                              x[0:whole * P, :].rearrange("(b p) f -> p b f", p=P)).then_inc(x_in, 16)
            if tail:
                act.dma_start(state[0:tail, whole * P:(whole + 1) * P], x[whole * P:n_nodes, :]).then_inc(x_in, 16)

            def normalise(into, ready, first, n):
                for b in range(n):
                    done = act.activation(into[:, b * P:(b + 1) * P], state[:, ds((first + b) * P, P)], ACT.Relu,
                                          bias=shift[:, ds(first + b, 1)], scale=rstd[:, ds(first + b, 1)])
                done.then_inc(ready, 1)

            act.wait_ge(variance_ready, 1)
            act.activation(spread[:, :], spread[:, :], ACT.Sqrt).then_inc(spread_ready, 1)
            act.wait_ge(norm_ready, 1)
            act.wait_ge(weights_in, 16 * 6)
            with act.Fori(0, pair_turns) as t:
                for i in range(2):
                    act.wait_ge(h_turned[i], t)
                    normalise(normed[i], h_ready[i], (t * 2 + i) * PAIR, PAIR)
                for i in range(2):
                    act.wait_ge(own_summed[i], t + 1)
                    act.activation(acc[:, ds((t * 2 + i) * (PAIR * P), PAIR * P)], banks[:, 2 + i, 0:PAIR * P],
                                   ACT.Identity, bias=b_own[:, 0:1]).then_inc(own_copied[i], 1)

            for k in range(1 + HOPS):
                index = index_typed if k == 0 else index_plain
                with act.Fori(0, turns) as t:
                    for j in range(SLOTS):
                        act.wait_ge(rows_landed[j], t * (16 * CHUNKS) + k * turns * 16 * CHUNKS)
                        act.copy(ring_index[:, j, :], index[:, ds((t * SLOTS + j) * CHUNKS, CHUNKS)]).then_inc(index_ready[j], 1)
                if k == 0:
                    act.wait_ge(prepared, 1)
                flag = act.value_load(rest_flag[0:1, 0:1], min_val=0, max_val=1)
                with act.If(flag > 0):
                    act.wait_ge(rows_landed[0], (k + 1) * turns * 16 * CHUNKS)
                    with act.Fori(0, groups) as g:
                        act.wait_ge(rest_landed, g * (16 * CHUNKS) + k * groups * 16 * CHUNKS)
                        act.copy(ring_index[:, 0, :], index[:, ds(g * CHUNKS, CHUNKS)]).then_inc(rest_index, 1)
                    act.nop()
                if k == 0:
                    act.wait_ge(degree_bounded, 1)
                    act.activation(spread[:, :], linked[:, :], ACT.Sqrt).then_inc(degree_root, 1)
                act.wait_ge(pass_done, k + 1)
                with act.Fori(0, five_turns) as t:
                    for i in range(2):
                        act.wait_ge(stage_turned[i], t + k * five_turns)
                        act.activation(staged[i], acc[:, ds((t * 2 + i) * batch, batch)],
                                       ACT.Relu if k == 0 else ACT.Copy).then_inc(stage_ready[i], 1)
                if k == 0:
                    act.wait_ge(variance_ready, 2)
                    act.activation(spread[:, :], spread[:, :], ACT.Sqrt).then_inc(spread_ready, 1)
                    act.wait_ge(norm_ready, 2)
                    with act.Fori(0, five_turns) as t:
                        for i in range(2):
                            act.wait_ge(fresh_used[i], t)
                            normalise(fresh[i], fresh_ready[i], (t * 2 + i) * FIVE, FIVE)

        @block.tensor
        def _(pe):
            pe.wait_ge(identity_made, 1)
            pe.wait_ge(edges_ready, 1)
            for k in range(tiles):
                if k >= 2:
                    pe.wait_ge(tile_copied, k - 1)
                for n, raw in enumerate((raw_type, raw_src, raw_dst[:, :].rearrange("p k e -> p (k e)"))):
                    last = pe.transpose(banks[:, k % 2, n * P:(n + 1) * P], raw.bitcast(F32)[:, k * P:(k + 1) * P], identity[:, :])
                last.then_inc(tile_turned, 1)
            pe.wait_ge(min_ready, 1)
            pe.transpose(banks[0:tiles, 2, 0:P], chunk_min[:, :], identity[:, :]).then_inc(min_turned, 1)
            pe.wait_ge(weights_in, 16 * 6)
            for n in range(3):
                last = pe.transpose(banks[:, 3, n * P:(n + 1) * P], weights[:, n, :], identity[:, :])
            last.then_inc(weights_turned, 1)
            pe.wait_ge(rest_ready, 1)
            pe.transpose(banks[0:1, 2, P:2 * P], rest_min[:, :], identity[:, :]).then_inc(rest_turned, 1)
            pe.wait_ge(zeroed, 2)
            pe.matmul(degree, zeros[:, 0:P], zeros[:, 0:blocks], start=True, stop=False, skip_group_check=True)

            pe.wait_ge(weights_copied, 1)
            with pe.Fori(0, pair_turns) as t:
                for i in range(2):
                    pe.wait_ge(h_ready[i], t + 1)
                    pe.wait_ge(h_copied[i], t)
                    for b in range(PAIR):
                        last = pe.transpose(banks[:, i, b * P:(b + 1) * P], normed[i][:, b * P:(b + 1) * P], identity[:, :])
                    last.then_inc(h_turned[i], 1)
                for i in range(2):
                    pe.wait_ge(h_copied[i], t + 1)
                    pe.wait_ge(message_ready[i], t)
                    for b in range(PAIR):
                        last = pe.matmul(typed_banks[:, i, b * 2 * P:(b + 1) * 2 * P], normed_t[i][:, b * P:(b + 1) * P],
                                         w_types[:, :], start=True, stop=True)
                    last.then_inc(typed_summed[i], 1)
                    pe.wait_ge(own_copied[i], t)
                    pe.matmul(banks[:, 2 + i, 0:PAIR * P], w_own[:, :], normed_t[i], start=True, stop=True
                              ).then_inc(own_summed[i], 1)

            def sums(bank, slot):
                for c in range(CHUNKS):
                    last = pe.matmul(bank, rows[:, slot, c, :], hot[:, slot, c, :], start=(c == 0), stop=(c == CHUNKS - 1))
                return last

            for k in range(1 + HOPS):
                with pe.Fori(0, turns) as t:
                    for j in range(SLOTS):
                        pe.wait_ge(hot_ready[j], t + (k * turns + 1))
                        pe.wait_ge(added[j], t + k * turns)
                        pe.wait_ge(rows_landed[j], t * (16 * CHUNKS) + (k * turns + 1) * 16 * CHUNKS)
                        sums(banks[:, j, 0:P], j).then_inc(summed[j], 1)
                        if k == 0:
                            i = j % 2
                            pe.wait_ge(degree_hot[i], t * (SLOTS // 2) + (j // 2 + 1))
                            for c in range(CHUNKS):
                                last = pe.matmul(degree, hot_row[:, i, c, :], hot_block[:, i, c, :],
                                                 start=False, stop=False, skip_group_check=True)
                            last.then_inc(degree_summed[i], 1)
                if k == 0:
                    pe.wait_ge(prepared, 1)
                flag = pe.value_load(rest_flag[0:1, 0:1], min_val=0, max_val=1)
                with pe.If(flag > 0):
                    pe.wait_ge(added[0], (k + 1) * turns)
                    with pe.Fori(0, groups) as g:
                        landed, = ready_early(pe, g * (16 * CHUNKS) + (k * groups + 1) * 16 * CHUNKS)
                        pe.wait_ge(added[0], (k + 1) * turns)
                        pe.wait_ge(rest_landed, landed)
                        with pe.Fori(0, blocks) as w:
                            pe.wait_ge(rest_hot, g * blocks + w + (k * rest_turns + 1))
                            pe.wait_ge(rest_added, g * blocks + w + k * rest_turns)
                            sums(banks[:, 0, 0:P], 0).then_inc(rest_summed, 1)
                    pe.nop()
                with pe.Fori(0, five_turns) as t:
                    for i in range(2):
                        pe.wait_ge(stage_ready[i], t + (k * five_turns + 1))
                        pe.wait_ge(turned_used[i], t + k * five_turns)
                        for b in range(FIVE):
                            last = pe.transpose(turned[i][:, b * P:(b + 1) * P], staged[i][:, b * P:(b + 1) * P], identity[:, :])
                        last.then_inc(stage_turned[i], 1)

        @block.vector
        def _(dve):
            chain = Steps(dve, step)
            done = chain.then_wait
            for raw, value in ((raw_src, 0), (raw_type, 0), (raw_dst[:, :].rearrange("p k e -> p (k e)"), FAR)):
                dve.memset(raw[:, (tiles - 1) * P:tiles * P], value).then_inc(padded_edges, 1)
            dve.memset(state[:, whole * P:padded], 0.0).then_inc(padded_x, 1)
            dve.wait_ge(iota_made, 1)
            done(dve.tensor_copy(count_up, iota[:, :]))
            dve.memset(acc[:, padded:padded + P], 0.0).then_inc(zeroed, 1)

            loads = 3 * ((tiles > 1) + (full_rows > 0) + (odd_edges > 0))
            dve.wait_ge(edges_in, 16 * loads)
            dst_flat = raw_dst[:, :].rearrange("p k e -> p (k e)")
            done(dve.tensor_copy(raw_src.bitcast(F32), raw_src))
            done(dve.tensor_scalar(raw_type.bitcast(F32), raw_type, 0.0, float(padded), ALU.not_equal, ALU.mult))
            dve.tensor_copy(dst_flat.bitcast(F32), dst_flat).then_inc(step, 1)
            done(dve.tensor_tensor(raw_type.bitcast(F32), raw_type.bitcast(F32), raw_src.bitcast(F32), ALU.add))
            chain.done += 1
            dve.wait_ge(step, chain.done)
            dve.tensor_reduce(chunk_min[:, :], raw_dst[:, :, :].bitcast(F32), AX_X, ALU.min).then_inc(edges_ready, 1)
            dve.wait_ge(edges_ready, 1)
            dve.engine_nop().then_inc(min_ready, 1)
            for k in range(tiles):
                columns = slice(k * P, (k + 1) * P)
                dve.wait_ge(tile_turned, k + 1)
                dve.tensor_copy(index_typed[:, columns], banks[:, k % 2, 0:P])
                dve.tensor_copy(index_plain[:, columns], banks[:, k % 2, P:2 * P])
                dve.tensor_copy(local[:, columns], banks[:, k % 2, 2 * P:3 * P])
                dve.tensor_copy(dst_row[:, columns], banks[:, k % 2, 2 * P:3 * P]).then_inc(tile_copied, 1)
            dve.wait_ge(min_turned, 1)
            done(dve.tensor_reduce(group_min[0:tiles, :], banks[0:tiles, 2, 0:P].rearrange("k (g c) -> k g c", c=CHUNKS),
                                   AX_X, ALU.min))
            dve.tensor_scalar(group_base[0:tiles, :], group_min[0:tiles, :], float(n_nodes - 1), 0.0, ALU.min, ALU.max
                              ).then_inc(base_made, 1)
            dve.wait_ge(weights_turned, 1)
            dve.tensor_copy(w_types[:, :], banks[:, 3, 0:2 * P])
            dve.tensor_copy(w_own[:, :], banks[:, 3, 2 * P:3 * P]).then_inc(weights_copied, 1)
            dve.wait_ge(tile_copied, tiles)
            done(dve.tensor_single_scalar(dst_block[:, :], dst_row[:, :], 7, ALU.logical_shift_right))
            done(dve.tensor_single_scalar(dst_row[:, :], dst_row[:, :], P - 1, ALU.bitwise_and))
            dve.wait_ge(base_in, 32)
            by_group = local[:, :].rearrange("p (g c) -> p g c", c=CHUNKS)
            bases = base_all[:, :].unsqueeze(2).to_broadcast([P, groups, CHUNKS])
            done(dve.tensor_copy(rest[:, :], local[:, :]))
            done(dve.tensor_tensor(by_group, by_group, bases, ALU.subtract))
            inside = raw_dst[:, :].rearrange("p k e -> p (k e)").bitcast(F32)
            done(dve.tensor_scalar(inside, local[:, :], float(P), float(FAR), ALU.is_lt, ALU.mult))
            done(dve.tensor_tensor(rest[:, :], rest[:, :], inside, ALU.max))
            dve.tensor_reduce(rest_min[:, :], rest[:, :], AX_X, ALU.min).then_inc(rest_ready, 1)
            dve.wait_ge(rest_turned, 1)
            done(dve.tensor_reduce(any_rest[0:1, :], banks[0:1, 2, P:2 * P], AX_X, ALU.min))
            dve.tensor_scalar(rest_flag[0:1, :], any_rest[0:1, :], float(n_nodes), None, ALU.is_lt).then_inc(prepared, 1)

            def norm(count):
                dve.tensor_scalar(spread[:, :], stats[:, :, 1], EPS, None, ALU.add).then_inc(variance_ready, 1)
                dve.wait_ge(spread_ready, count)
                done(dve.reciprocal(rstd[:, :], spread[:, :]))
                dve.scalar_tensor_tensor(out=shift[:, :], in0=stats[:, :, 0], scalar=-1.0, in1=rstd[:, :],
                                         op0=ALU.mult, op1=ALU.mult).then_inc(norm_ready, 1)

            def statistics(first, slot, n):
                for b in range(n):
                    last = dve.bn_stats(bn[:, slot * n + b, :], state[:, ds((first + b) * P, P)])
                done(last, also=(x_in, 16))
                for b in range(n):
                    last = dve.bn_aggr(moments[:, slot * n + b, :], bn[:, slot * n + b, :])
                done(last)
                done(dve.tensor_copy(stats[:, ds(first, n), :], moments[:, slot * n:(slot + 1) * n, :]))

            dve.wait_ge(x_in, 16 * ((whole > 0) + (tail > 0)))
            with dve.Fori(0, five_turns) as t:
                chain.enter(t, 6)
                for i in range(2):
                    statistics((t * 2 + i) * FIVE, i, FIVE)
            chain.leave(five_turns)
            norm(1)
            biases = b_types[:, :].unsqueeze(1).to_broadcast([P, PAIR, 2 * P])
            with dve.Fori(0, pair_turns) as t:
                for i in range(2):
                    dve.wait_ge(own_summed[i], t)
                    dve.wait_ge(h_turned[i], t + 1)
                    dve.tensor_copy(normed_t[i], banks[:, i, 0:PAIR * P]).then_inc(h_copied[i], 1)
                for i in range(2):
                    dve.wait_ge(message_stored[i], t * 32)
                    dve.wait_ge(typed_summed[i], t + 1)
                    dve.tensor_tensor(messages[i].rearrange("p (b f) -> p b f", b=PAIR),
                                      typed_banks[:, i, :].rearrange("p (b f) -> p b f", b=PAIR), biases, ALU.add
                                      ).then_inc(message_ready[i], 1)

            for i in range(2):
                dve.wait_ge(own_copied[i], pair_turns)
            for k in range(1 + HOPS):
                if k:
                    dve.wait_ge(acc_cleared, k * 2 * five_turns)
                with dve.Fori(0, turns) as t:
                    for j in range(SLOTS):
                        group = t * SLOTS + j
                        base = dve.value_load(base_row[0:1, ds(group, 1)], min_val=0, max_val=n_nodes - 1)
                        dve.wait_ge(summed[j], t + k * turns)
                        dve.tensor_tensor(hot[:, j, :, :], counting(P), over_hot(local[:, ds(group * CHUNKS, CHUNKS)], P),
                                          ALU.is_equal).then_inc(hot_ready[j], 1)
                        if k == 0:
                            i = j % 2
                            dve.wait_ge(degree_summed[i], t * (SLOTS // 2) + j // 2)
                            dve.tensor_tensor(hot_row[:, i, :, :], counting(P),
                                              over_hot(dst_row[:, ds(group * CHUNKS, CHUNKS)], P), ALU.is_equal)
                            dve.tensor_tensor(hot_block[:, i, :, :], counting(blocks),
                                              over_hot(dst_block[:, ds(group * CHUNKS, CHUNKS)], blocks),
                                              ALU.is_equal).then_inc(degree_hot[i], 1)
                        dve.wait_ge(added[j - 1], t + (k * turns + (j > 0)))
                        dve.wait_ge(summed[j], t + (k * turns + 1))
                        into = acc[:, ds(base, P)]
                        dve.tensor_tensor(into, banks[:, j, 0:P], into, ALU.add).then_inc(added[j], 1)
                dve.wait_ge(added[SLOTS - 1], (k + 1) * turns)
                flag = dve.value_load(rest_flag[0:1, 0:1], min_val=0, max_val=1)
                with dve.If(flag > 0):
                    with dve.Fori(0, groups) as g:
                        steps = g * (blocks + 1) + k * groups * (blocks + 1)
                        dve.wait_ge(rest_hot, g * blocks + k * rest_turns)
                        dve.wait_ge(rest_step, steps)
                        dve.tensor_copy(window[:, :], rest[:, ds(g * CHUNKS, CHUNKS)]).then_inc(rest_step, 1)
                        with dve.Fori(0, blocks) as w:
                            dve.wait_ge(rest_step, steps + w + 1)
                            dve.wait_ge(rest_summed, g * blocks + w + k * rest_turns)
                            dve.tensor_tensor(hot[:, 0, :, :], counting(P), over_hot(window[:, :], P),
                                              ALU.is_equal).then_inc(rest_hot, 1)
                            dve.wait_ge(rest_hot, g * blocks + w + (k * rest_turns + 1))
                            dve.tensor_scalar(window[:, :], window[:, :], float(P), None, ALU.subtract).then_inc(rest_step, 1)
                            dve.wait_ge(rest_added, g * blocks + w + k * rest_turns)
                            dve.wait_ge(rest_summed, g * blocks + w + (k * rest_turns + 1))
                            into = acc[:, ds(w * P, P)]
                            dve.tensor_tensor(into, banks[:, 0, 0:P], into, ALU.add).then_inc(rest_added, 1)
                    dve.wait_ge(rest_added, (k + 1) * rest_turns)
                dve.engine_nop().then_inc(pass_done, 1)

                if k == 0:
                    for i in range(2):
                        dve.wait_ge(degree_summed[i], turns * (SLOTS // 2))
                    dve.tensor_scalar(linked[:, :], degree, 1.0, None, ALU.max).then_inc(degree_bounded, 1)
                    dve.wait_ge(degree_root, 1)
                    done(dve.reciprocal(inv[:, :], spread[:, :]))
                    done(dve.tensor_scalar(linked[:, :], degree, 0.0, None, ALU.is_gt))
                    done(dve.tensor_tensor(inv[:, :], inv[:, :], linked[:, :], ALU.mult))
                    done(dve.tensor_scalar(inv_third[:, :], inv[:, :], 1.0 / (HOPS + 1), None, ALU.mult))
                    with dve.Fori(0, five_turns) as t:
                        chain.enter(t, 6)
                        for i in range(2):
                            part = state[:, ds((t * 2 + i) * batch, batch)]
                            dve.wait_ge(stage_turned[i], t + 1)
                            dve.tensor_tensor(part, turned[i], part, ALU.add).then_inc(turned_used[i], 1)
                            dve.wait_ge(turned_used[i], t + 1)
                            statistics((t * 2 + i) * FIVE, i, FIVE)
                    chain.leave(five_turns)
                    norm(2)
                    with dve.Fori(0, five_turns) as t:
                        for i in range(2):
                            part = state[:, ds((t * 2 + i) * batch, batch)]
                            dve.wait_ge(scaled_stored[i], t * 16)
                            dve.wait_ge(fresh_ready[i], t + 1)
                            dve.tensor_tensor(blocks_of(scaled[i], FIVE), blocks_of(fresh[i], FIVE),
                                              over_features(inv[:, ds((t * 2 + i) * FIVE, FIVE)], FIVE), ALU.mult
                                              ).then_inc(scaled_ready[i], 1)
                            dve.scalar_tensor_tensor(out=part, in0=fresh[i], scalar=1.0 / (HOPS + 1), in1=part,
                                                     op0=ALU.mult, op1=ALU.add).then_inc(fresh_used[i], 1)
                elif k < HOPS:
                    with dve.Fori(0, five_turns) as t:
                        for i in range(2):
                            part = state[:, ds((t * 2 + i) * batch, batch)]
                            factors = over_features(inv[:, ds((t * 2 + i) * FIVE, FIVE)], FIVE)
                            dve.wait_ge(stage_turned[i], t + (k * five_turns + 1))
                            dve.tensor_tensor(blocks_of(fresh[i], FIVE), blocks_of(turned[i], FIVE), factors,
                                              ALU.mult).then_inc(turned_used[i], 1)
                            dve.wait_ge(turned_used[i], t + (k * five_turns + 1))
                            dve.wait_ge(scaled_stored[i], t * 16 + k * five_turns * 16)
                            dve.tensor_tensor(blocks_of(scaled[i], FIVE), blocks_of(fresh[i], FIVE), factors,
                                              ALU.mult).then_inc(scaled_ready[i], 1)
                            dve.scalar_tensor_tensor(out=part, in0=fresh[i], scalar=1.0 / (HOPS + 1), in1=part,
                                                     op0=ALU.mult, op1=ALU.add).then_inc(fresh_used[i], 1)
                else:
                    with dve.Fori(0, five_turns) as t:
                        for i in range(2):
                            part = state[:, ds((t * 2 + i) * batch, batch)]
                            dve.wait_ge(stage_turned[i], t + (k * five_turns + 1))
                            dve.tensor_tensor(blocks_of(fresh[i], FIVE), blocks_of(turned[i], FIVE),
                                              over_features(inv_third[:, ds((t * 2 + i) * FIVE, FIVE)], FIVE), ALU.mult
                                              ).then_inc(turned_used[i], 1)
                            dve.wait_ge(turned_used[i], t + (k * five_turns + 1))
                            dve.wait_ge(scaled_stored[i], t * 16 + k * five_turns * 16)
                            dve.tensor_tensor(scaled[i], fresh[i], part, ALU.add).then_inc(scaled_ready[i], 1)


_INS = ["x", "src", "dst", "edge_type_2", "L0_gnn_W_data", "L0_gnn_b_data", "L0_gnn_W_control",
        "L0_gnn_b_control", "L0_gnn_W_self", "L0_gnn_b_self"]


def kernel(**inputs):
    import numpy as _np
    import concourse.bacc as _bacc
    from concourse.bass_utils import run_bass_kernel_spmd as _run

    nc = _bacc.Bacc("TRN2", target_bir_lowering=False, num_devices=1)
    arrays, args = {}, []
    for name in _INS:
        a = _np.ascontiguousarray(inputs[name])
        arrays[f"in_{name}"] = a
        args.append(nc.dram_tensor(f"in_{name}", a.shape, mybir.dt.from_np(a.dtype), kind="ExternalInput").ap())
    out = nc.dram_tensor("out", arrays["in_x"].shape, F32, kind="ExternalOutput").ap()
    gnn_kernel(nc, *args, out)
    r = _run(nc, [arrays], core_ids=[0])
    return r.results[0]["out"]
```

```python
from contextlib import ExitStack

import concourse.bass as bass
from concourse import mybir

P = 128
CHUNKS = 8
GROUP = CHUNKS * P
TILE_GROUPS = P // CHUNKS
SLOTS = 4
PAIR = 2
FIVE = 5
LEAD = 2
AHEAD = 1
SPAN = 8
PARTS = ((0, 3), (3, 6), (6, 8))
BATCHES = len(PARTS)
LOADS = 5
FAR = 1 << 20
EPS = 1e-5
HOPS = 2

F32 = mybir.dt.float32
BF16 = mybir.dt.bfloat16
I32 = mybir.dt.int32
ALU = mybir.AluOpType
ACT = mybir.ActivationFunctionType
AX_X = mybir.AxisListType.X
ds = bass.ds


class Steps:

    def __init__(self, engine, semaphore):
        self.engine, self.semaphore, self.start, self.done = engine, semaphore, 0, 0

    def begin(self, start):
        self.start, self.done = start, 0

    def then_wait(self, instruction):
        instruction.then_inc(self.semaphore, 1)
        self.done += 1
        self.engine.wait_ge(self.semaphore, self.start + self.done)


def ready_early(engine, *values):
    for value in values:
        engine.compute_val(value)
    return values


def gnn_kernel(nc, x, src, dst, edge_type, w_data, b_data, w_control, b_control, w_self, b_self, out):
    n_nodes, features = x.shape
    n_edges = src.shape[0]
    assert features == P

    batch = FIVE * P
    padded = -(-n_nodes // (2 * batch)) * 2 * batch
    while padded % (2 * PAIR * P):
        padded += 2 * batch
    blocks = padded // P
    whole = n_nodes // P
    tail = n_nodes - whole * P
    pair_turns = blocks // (2 * PAIR)
    total = blocks // FIVE
    load = blocks // LOADS
    assert n_nodes > padded - batch and blocks <= P and blocks % LOADS == 0 and load % FIVE == 0

    tiles = -(-n_edges // (P * P))
    chunks = tiles * P
    groups = tiles * TILE_GROUPS
    turns = groups // SLOTS
    last_edge = (tiles - 1) * P * P
    full_rows = (n_edges - last_edge) // P
    odd_edges = n_edges - last_edge - full_rows * P

    spans = (turns - LEAD - AHEAD) // SPAN
    late = list(range(spans * BATCHES, total))
    slope = BATCHES * batch // (SPAN * SLOTS)
    assert late and all((n + 1) * batch <= slope * SLOTS * after for n, (_, after) in enumerate(PARTS))

    typed_table = nc.dram_tensor("typed_table", (2 * padded, P), F32, kind="Internal").ap()
    tables = [typed_table] + [nc.dram_tensor(f"hop_table{n}", (padded, P), F32, kind="Internal").ap() for n in range(HOPS)]
    base_dram = nc.dram_tensor("base_dram", (1, groups), I32, kind="Internal").ap()

    with ExitStack() as ctx:
        def sbuf(name, shape, dtype=F32):
            return ctx.enter_context(nc.sbuf_tensor(name, [P, *shape], dtype))

        def semaphore(name):
            return ctx.enter_context(nc.semaphore(name))

        def semaphores(name, n):
            return [semaphore(f"{name}{i}") for i in range(n)]

        state = sbuf("state", [padded])
        acc = sbuf("acc", [padded + P])
        index = sbuf("index", [2, chunks], I32)
        local = sbuf("local", [chunks])
        rest = sbuf("rest", [chunks])
        dst_block = sbuf("dst_block", [chunks], I32)
        dst_row = sbuf("dst_row", [chunks], I32)
        rows = sbuf("rows", [SLOTS, CHUNKS, P])
        hot = sbuf("hot", [SLOTS, CHUNKS, P])
        ring_index = sbuf("ring_index", [SLOTS, CHUNKS], I32)
        hot_row = sbuf("hot_row", [2, CHUNKS, P], BF16)
        hot_block = sbuf("hot_block", [2, CHUNKS, blocks], BF16)
        staged = sbuf("staged", [batch])
        fresh = sbuf("fresh", [batch])
        scaled = sbuf("scaled", [batch])
        zeros = sbuf("zeros", [P])
        iota = sbuf("iota", [P], I32)
        identity = sbuf("identity", [P])
        weights = sbuf("weights", [3, P])
        w_types = sbuf("w_types", [2 * P])
        w_own = sbuf("w_own", [P])
        b_types = sbuf("b_types", [2 * P])
        b_own = sbuf("b_own", [1])
        bn = sbuf("bn", [blocks, 6])
        means = sbuf("means", [blocks])
        skew = sbuf("skew", [blocks])
        squares = sbuf("squares", [blocks])
        spread = sbuf("spread", [blocks])
        rstd = sbuf("rstd", [blocks])
        shift = sbuf("shift", [blocks])
        batch_spread = sbuf("batch_spread", [2, FIVE])
        batch_rstd = sbuf("batch_rstd", [2, FIVE])
        batch_shift = sbuf("batch_shift", [FIVE])
        linked = sbuf("linked", [FIVE])
        inv = sbuf("inv", [blocks])
        inv_third = sbuf("inv_third", [blocks])
        chunk_min = sbuf("chunk_min", [tiles])
        group_min = sbuf("group_min", [TILE_GROUPS])
        group_base = sbuf("group_base", [TILE_GROUPS], I32)
        line = sbuf("line", [TILE_GROUPS], I32)
        above = sbuf("above", [TILE_GROUPS])
        above_min = sbuf("above_min", [1])
        base_row = sbuf("base_row", [groups], I32)
        base_all = sbuf("base_all", [groups], I32)
        rest_min = sbuf("rest_min", [1])
        checks = sbuf("checks", [4])
        uneven = sbuf("uneven", [1], I32)
        window = sbuf("window", [CHUNKS])

        raw_src = hot[:, 0:2].rearrange("p s c f -> p (s c f)")[:, 0:chunks].bitcast(I32)
        raw_type = hot[:, 2:4].rearrange("p s c f -> p (s c f)")[:, 0:chunks].bitcast(I32)
        raw_dst = dst_block[:, :]
        flat = rows[:, :].rearrange("p s c f -> p (s c f)")

        def carve(start, size):
            return [flat[:, start + i * size:start + (i + 1) * size] for i in range(2)]

        normed = carve(0, PAIR * P)
        normed_t = carve(2 * PAIR * P, PAIR * P)
        messages = carve(4 * PAIR * P, 2 * PAIR * P)
        assert chunks <= 2 * GROUP

        def bank(name, n):
            return ctx.enter_context(nc.psum_tensor(name, [P, n, 512], F32))

        sums_bank = bank("sums_bank", 2)
        turned_bank = bank("turned_bank", 2)
        own_bank = bank("own_bank", 2)
        degree = bank("degree", 1)[:, 0, 0:blocks]
        count_up = bank("count_up", 1)[:, 0, 0:P]
        turned = turned_bank[:, :, :].rearrange("p a f -> p (a f)")[:, 0:batch]
        own = own_bank[:, :, :].rearrange("p a f -> p (a f)")[:, 0:batch]

        src_in = semaphore("src_in")
        type_in = semaphore("type_in")
        dst_in = semaphore("dst_in")
        weights_in = semaphore("weights_in")
        x_in = semaphores("x_in", LOADS)
        padded_edges = semaphore("padded_edges")
        padded_x = semaphore("padded_x")
        zeroed = semaphore("zeroed")
        iota_made = semaphore("iota_made")
        line_made = semaphore("line_made")
        count_made = semaphore("count_made")
        identity_made = semaphore("identity_made")
        weights_turned = semaphore("weights_turned")
        weights_copied = semaphore("weights_copied")
        pool_step = semaphore("pool_step")
        sources_ready = semaphore("sources_ready")
        dst_ready = semaphore("dst_ready")
        index_turned = semaphore("index_turned")
        index_copied = semaphore("index_copied")
        dst_turned = semaphore("dst_turned")
        dst_copied = semaphore("dst_copied")
        min_ready = semaphore("min_ready")
        min_turned = semaphore("min_turned")
        base_made = semaphore("base_made")
        base_stored = semaphore("base_stored")
        base_in = semaphore("base_in")
        rest_ready = semaphore("rest_ready")
        rest_turned = semaphore("rest_turned")
        prepared = semaphore("prepared")
        x_measured = semaphore("x_measured")
        variance_ready = semaphore("variance_ready")
        spread_ready = semaphore("spread_ready")
        norm_ready = semaphore("norm_ready")
        h_ready = semaphores("h_ready", 2)
        h_turned = semaphores("h_turned", 2)
        h_copied = semaphores("h_copied", 2)
        typed_summed = semaphores("typed_summed", 2)
        message_ready = semaphores("message_ready", 2)
        message_stored = semaphores("message_stored", 2)
        index_ready = semaphores("index_ready", SLOTS)
        rows_landed = semaphores("rows_landed", SLOTS)
        hot_ready = semaphores("hot_ready", SLOTS)
        summed = semaphores("summed", SLOTS)
        added = semaphores("added", SLOTS)
        degree_hot = semaphores("degree_hot", 2)
        degree_summed = semaphores("degree_summed", 2)
        degree_read = semaphore("degree_read")
        own_h = semaphore("own_h")
        own_turned = semaphore("own_turned")
        own_staged = semaphore("own_staged")
        own_summed = semaphore("own_summed")
        own_added = semaphore("own_added")
        stage_ready = semaphore("stage_ready")
        acc_cleared = semaphore("acc_cleared")
        stage_turned = semaphore("stage_turned")
        turned_used = semaphore("turned_used")
        batch_variance = semaphore("batch_variance")
        batch_root = semaphore("batch_root")
        batch_norm = semaphore("batch_norm")
        fresh_ready = semaphore("fresh_ready")
        fresh_used = semaphore("fresh_used")
        scaled_ready = semaphore("scaled_ready")
        scaled_stored = semaphore("scaled_stored")
        step = semaphore("step")
        batch_step = semaphore("batch_step")
        rest_index = semaphore("rest_index")
        rest_landed = semaphore("rest_landed")
        rest_hot = semaphore("rest_hot")
        rest_summed = semaphore("rest_summed")
        rest_added = semaphore("rest_added")
        rest_step = semaphore("rest_step")

        rest_turns = groups * blocks

        def in_blocks(ap, n=FIVE):
            return ap.rearrange("p (b f) -> p b f", b=n)

        def over_features(ap):
            return ap.unsqueeze(2).to_broadcast([P, FIVE, P])

        def over_hot(ap, columns):
            return ap.unsqueeze(2).to_broadcast([P, CHUNKS, columns])

        def counting(columns):
            return count_up[:, 0:columns].unsqueeze(1).to_broadcast([P, CHUNKS, columns])

        def table_rows(table, first, n):
            return table[ds(first, n * P), :].rearrange("(b p) f -> p b f", p=P)

        def one_pass(engine, k, turn, own_step, finish, outside, ahead=0):
            lead = LEAD + ahead
            with engine.Fori(0, lead) as t:
                turn(k, t)
            if k == 0:
                for nth, s in enumerate(late):
                    own_step(s, nth, 0)
                engine.wait_ge(prepared, 1)
            flag = engine.value_load(uneven[0:1, 0:1], min_val=0, max_val=1)
            with engine.If(flag > 0):
                if k == 0:
                    with engine.Fori(0, spans * BATCHES) as s:
                        own_step(s, s + len(late), 0)
                with engine.Fori(lead, turns) as t:
                    turn(k, t)
                outside(k)
                with engine.Fori(0, total) as s:
                    finish(k, s, turns, total)
                engine.nop()
            with engine.Else():
                with engine.Fori(0, spans) as q:
                    for r, (start, end) in enumerate(PARTS):
                        with engine.Fori(start, end) as u:
                            turn(k, q * SPAN + u + lead)
                        if k == 0:
                            own_step(q * BATCHES + r, q * BATCHES + (r + len(late)), q * BATCHES + r)
                        finish(k, q * BATCHES + r, q * SPAN + (LEAD + end), q * BATCHES + (r + 1 + len(late)))
                if lead + spans * SPAN < turns:
                    with engine.Fori(lead + spans * SPAN, turns) as t:
                        turn(k, t)
                for s in late:
                    finish(k, s, turns, total)
                engine.nop()

        def nothing(*_):
            pass

        block = ctx.enter_context(nc.Block())

        @block.sync
        def _(sp):
            def edges(raw, array, landed):
                by_tile = raw.rearrange("p (k e) -> p k e", k=tiles)
                if tiles > 1:
                    sp.dma_start(by_tile[:, 0:tiles - 1, :],
                                 array[0:last_edge].rearrange("(k p e) -> p k e", p=P, e=P)).then_inc(landed, 16)
                if full_rows:
                    sp.dma_start(by_tile[0:full_rows, tiles - 1, :],
                                 array[last_edge:last_edge + full_rows * P].rearrange("(p e) -> p e", e=P)
                                 ).then_inc(landed, 16)
                if odd_edges:
                    sp.dma_start(by_tile[full_rows:full_rows + 1, tiles - 1, 0:odd_edges],
                                 array[n_edges - odd_edges:n_edges].rearrange("(p e) -> p e", p=1)
                                 ).then_inc(landed, 16)

            def nodes(n):
                first, end = n * load, min((n + 1) * load, whole)
                if end > first:
                    sp.dma_start(in_blocks(state[:, first * P:end * P], end - first),
                                 x[first * P:end * P, :].rearrange("(b p) f -> p b f", p=P)).then_inc(x_in[n], 16)
                if tail and n * load <= whole < (n + 1) * load:
                    sp.dma_start(state[0:tail, whole * P:(whole + 1) * P], x[whole * P:n_nodes, :]).then_inc(x_in[n], 16)

            sp.wait_ge(padded_x, 1)
            nodes(0)
            nodes(1)
            sp.wait_ge(padded_edges, 3)
            edges(raw_src, src, src_in)
            edges(raw_type, edge_type, type_in)
            for n in range(2, LOADS):
                nodes(n)
            edges(raw_dst, dst, dst_in)
            with sp.Fori(0, pair_turns) as t:
                for i in range(2):
                    first = (t * 2 + i) * (PAIR * P)
                    sp.wait_ge(message_ready[i], t + 1)
                    by_type = messages[i].rearrange("p (b k f) -> p b k f", b=PAIR, k=2)
                    for k in range(2):
                        sp.dma_start(table_rows(typed_table, first + k * padded, PAIR), by_type[:, :, k, :]
                                     ).then_inc(message_stored[i], 16)
            sp.wait_ge(base_made, 1)
            sp.dma_start(base_dram.rearrange("a (k g) -> (a k) g", k=tiles), group_base[0:tiles, :]).then_inc(base_stored, 16)
            sp.wait_ge(base_stored, 16)
            sp.dma_start(base_all[:, :], base_dram[0, :].partition_broadcast(P)).then_inc(base_in, 16)
            sp.dma_start(base_row[0:1, :], base_dram).then_inc(base_in, 16)
            for k in range(HOPS):
                with sp.Fori(0, total) as s:
                    sp.wait_ge(scaled_ready, s + (k * total + 1))
                    sp.dma_start(table_rows(tables[k + 1], s * batch, FIVE), in_blocks(scaled[:, :])).then_inc(scaled_stored, 16)
            full = n_nodes // batch
            with sp.Fori(0, full) as s:
                sp.wait_ge(scaled_ready, s + (HOPS * total + 1))
                sp.dma_start(out[ds(s * batch, batch), :].rearrange("(b p) f -> p b f", p=P), in_blocks(scaled[:, :])
                             ).then_inc(scaled_stored, 16)
            stored = HOPS * total + full
            if n_nodes % batch:
                sp.wait_ge(scaled_ready, stored + 1)
                n = whole - full * FIVE
                if n:
                    sp.dma_start(out[full * batch:whole * P, :].rearrange("(b p) f -> p b f", p=P),
                                 in_blocks(scaled[:, :])[:, 0:n, :]).then_inc(scaled_stored, 16)
                    stored += 1
                if tail:
                    sp.dma_start(out[whole * P:n_nodes, :], in_blocks(scaled[:, :])[0:tail, n, :]).then_inc(scaled_stored, 16)
                    stored += 1
            sp.wait_ge(scaled_stored, 16 * stored)

        @block.gpsimd
        def _(pool):
            pool.memset(zeros[:, :], 0.0).then_inc(zeroed, 1)
            pool.memset(identity[:, :], 0.0).then_inc(zeroed, 1)
            pool.iota(iota[:, :], pattern=[[1, P]], base=0, channel_multiplier=0).then_inc(iota_made, 1)
            pool.iota(line[:, :], pattern=[[-slope, TILE_GROUPS]], base=slope * SLOTS * LEAD,
                      channel_multiplier=-slope * TILE_GROUPS).then_inc(line_made, 1)
            pool.wait_ge(zeroed, 2)
            pool.affine_select(out=identity[:, :], in_=identity[:, :], compare_op=ALU.not_equal, fill=1.0,
                               base=0, pattern=[[-1, P]], channel_multiplier=1).then_inc(identity_made, 1)
            pool.memset(acc[:, :], 0.0).then_inc(zeroed, 1)
            arrivals = 16 * ((tiles > 1) + (full_rows > 0) + (odd_edges > 0))
            src_f, type_f, dst_f = (raw.bitcast(F32) for raw in (raw_src, raw_type, raw_dst))
            pool.wait_ge(src_in, arrivals)
            pool.tensor_copy(src_f, raw_src).then_inc(pool_step, 1)
            pool.wait_ge(type_in, arrivals)
            pool.tensor_copy(type_f, raw_type).then_inc(pool_step, 1)
            pool.wait_ge(pool_step, 2)
            pool.tensor_scalar(type_f, type_f, 0.0, -float(padded), ALU.is_equal, ALU.mult).then_inc(pool_step, 1)
            pool.wait_ge(pool_step, 3)
            pool.tensor_scalar(type_f, type_f, float(padded), None, ALU.add).then_inc(pool_step, 1)
            pool.wait_ge(pool_step, 4)
            pool.tensor_tensor(type_f, type_f, src_f, ALU.add).then_inc(sources_ready, 1)
            pool.wait_ge(dst_in, arrivals)
            pool.tensor_copy(dst_f, raw_dst).then_inc(dst_ready, 1)

            def gather(table, landed, slot):
                for c in range(CHUNKS):
                    pool.indirect_dma_start(
                        out=rows[:, slot, c, :], out_offset=None, in_=table,
                        in_offset=bass.IndirectOffsetOnAxis(ap=ring_index[:, slot, c:c + 1], axis=0)).then_inc(landed, 16)

            def stored(k, i):
                return (message_stored[i], 32 * pair_turns) if k == 0 else (scaled_stored, 16 * k * total)

            def turn(k, t):
                for j in range(SLOTS):
                    uses, before = ready_early(pool, t + (k * turns + 1), t + k * turns)
                    pool.wait_ge(*stored(k, 0))
                    pool.wait_ge(index_ready[j], uses)
                    pool.wait_ge(summed[j], before)
                    gather(tables[k], rows_landed[j], j)

            def outside(k):
                pool.wait_ge(summed[0], (k + 1) * turns)
                with pool.Fori(0, groups) as g:
                    uses, before = ready_early(pool, g + (k * groups + 1), g * blocks + k * rest_turns)
                    pool.wait_ge(*stored(k, 0))
                    pool.wait_ge(rest_index, uses)
                    pool.wait_ge(rest_summed, before)
                    gather(tables[k], rest_landed, 0)

            for k in range(1 + HOPS):
                pool.wait_ge(*stored(k, 1))
                one_pass(pool, k, turn, nothing, nothing, outside)

        @block.scalar
        def _(act):
            for n, w in enumerate((w_data, w_control, w_self)):
                act.dma_start(weights[:, n, :], w).then_inc(weights_in, 16)
            act.dma_start(b_types[:, 0:P], b_data.partition_broadcast(P)).then_inc(weights_in, 16)
            act.dma_start(b_types[:, P:2 * P], b_control.partition_broadcast(P)).then_inc(weights_in, 16)
            act.dma_start(b_own[:, :], b_self.rearrange("(p a) -> p a", a=1)).then_inc(weights_in, 16)
            for k in range(tiles):
                act.wait_ge(index_turned, k + 1)
                act.copy(index[:, :, k * P:(k + 1) * P], own_bank[:, k % 2, 0:2 * P].rearrange("p (a c) -> p a c", a=2)
                         ).then_inc(index_copied, 1)
            act.wait_ge(variance_ready, 1)
            act.activation(spread[:, :], spread[:, :], ACT.Sqrt).then_inc(spread_ready, 1)

            def normalise(into, block, scale, bias, n):
                for b in range(n):
                    last = act.activation(into[:, b * P:(b + 1) * P], state[:, ds((block + b) * P, P)], ACT.Relu,
                                          bias=bias(b), scale=scale(b))
                return last

            def normalise_x(into, block, n):
                return normalise(into, block, lambda b: rstd[:, ds(block + b, 1)], lambda b: shift[:, ds(block + b, 1)], n)

            act.wait_ge(norm_ready, 1)
            with act.Fori(0, pair_turns) as t:
                for i in range(2):
                    act.wait_ge(h_turned[i], t)
                    normalise_x(normed[i], (t * 2 + i) * PAIR, PAIR).then_inc(h_ready[i], 1)
                for i in range(2):
                    act.wait_ge(typed_summed[i], t)
                    act.wait_ge(h_turned[i], t + 1)
                    act.copy(normed_t[i], turned_bank[:, i, 0:PAIR * P]).then_inc(h_copied[i], 1)

            def turn(k, t):
                for j in range(SLOTS):
                    act.wait_ge(rows_landed[j], t * (16 * CHUNKS) + k * turns * 16 * CHUNKS)
                    act.copy(ring_index[:, j, :], index[:, min(k, 1), ds((t * SLOTS + j) * CHUNKS, CHUNKS)]
                             ).then_inc(index_ready[j], 1)

            def own_step(s, nth, finished):
                act.wait_ge(own_turned, nth)
                act.wait_ge(fresh_used, finished)
                normalise_x(fresh, s * FIVE, FIVE).then_inc(own_h, 1)
                act.wait_ge(own_turned, nth + 1)
                act.wait_ge(own_summed, nth)
                act.copy(staged[:, :], own).then_inc(own_staged, 1)

            def finish(k, s, after, owned):
                part = acc[:, ds(s * batch, batch)]
                act.wait_ge(added[SLOTS - 1], after + k * turns)
                act.wait_ge(stage_turned, s + k * total)
                if k == 0:
                    act.wait_ge(own_added, owned)
                act.activation(staged[:, :], part, ACT.Relu if k == 0 else ACT.Copy).then_inc(stage_ready, 1)
                if k < HOPS:
                    act.wait_ge(stage_ready, s + (k * total + 1))
                    part = acc[:, ds(act.compute_val(s * batch), batch)]
                    act.copy(part, zeros[:, 0:1].to_broadcast([P, batch])).then_inc(acc_cleared, 1)
                if k == 0:
                    act.wait_ge(batch_variance, s + 1)
                    act.activation(batch_spread[:, :, :], batch_spread[:, :, :], ACT.Sqrt).then_inc(batch_root, 1)
                    act.wait_ge(norm_ready, 1)
                    act.wait_ge(batch_norm, s + 1)
                    act.wait_ge(fresh_used, s)
                    normalise(fresh, s * FIVE, lambda b: batch_rstd[:, 0, b:b + 1], lambda b: batch_shift[:, b:b + 1], FIVE
                              ).then_inc(fresh_ready, 1)

            def outside(k):
                act.wait_ge(rows_landed[0], (k + 1) * turns * 16 * CHUNKS)
                with act.Fori(0, groups) as g:
                    act.wait_ge(rest_landed, g * (16 * CHUNKS) + k * groups * 16 * CHUNKS)
                    act.copy(ring_index[:, 0, :], index[:, min(k, 1), ds(g * CHUNKS, CHUNKS)]).then_inc(rest_index, 1)
                act.wait_ge(rest_added, (k + 1) * rest_turns)

            for k in range(1 + HOPS):
                one_pass(act, k, turn, own_step, finish, outside, AHEAD)

        @block.tensor
        def _(pe):
            pe.wait_ge(identity_made, 1)
            pe.wait_ge(weights_in, 16 * 6)
            for n in range(3):
                last = pe.transpose(turned_bank[:, 0, n * P:(n + 1) * P], weights[:, n, :], identity[:, :])
            last.then_inc(weights_turned, 1)
            pe.matmul(degree, zeros[:, :], zeros[:, 0:blocks], start=True, stop=False, skip_group_check=True)
            pe.wait_ge(sources_ready, 1)
            for k in range(tiles):
                if k >= 2:
                    pe.wait_ge(index_copied, k - 1)
                for n, raw in enumerate((raw_type, raw_src)):
                    last = pe.transpose(own_bank[:, k % 2, n * P:(n + 1) * P], raw.bitcast(F32)[:, k * P:(k + 1) * P], identity[:, :])
                last.then_inc(index_turned, 1)
            pe.wait_ge(weights_copied, 1)
            with pe.Fori(0, pair_turns) as t:
                for i in range(2):
                    pe.wait_ge(h_ready[i], t + 1)
                    pe.wait_ge(h_copied[i], t)
                    for b in range(PAIR):
                        last = pe.transpose(turned_bank[:, i, b * P:(b + 1) * P], normed[i][:, b * P:(b + 1) * P], identity[:, :])
                    last.then_inc(h_turned[i], 1)
                for i in range(2):
                    pe.wait_ge(h_copied[i], t + 1)
                    pe.wait_ge(message_ready[i], t)
                    for b in range(PAIR):
                        last = pe.matmul(sums_bank[:, i, b * 2 * P:(b + 1) * 2 * P], normed_t[i][:, b * P:(b + 1) * P],
                                         w_types[:, :], start=True, stop=True)
                    last.then_inc(typed_summed[i], 1)
            pe.wait_ge(index_copied, tiles)
            pe.wait_ge(min_ready, 1)
            pe.transpose(turned_bank[0:tiles, 0, 0:P], chunk_min[:, :], identity[:, :]).then_inc(min_turned, 1)
            for n in range(0, tiles, 4):
                if n >= 8:
                    pe.wait_ge(dst_copied, n // 4 - 1)
                for k in range(n, min(n + 4, tiles)):
                    last = pe.transpose(own_bank[:, n // 4 % 2, (k - n) * P:(k - n + 1) * P],
                                        raw_dst.bitcast(F32)[:, k * P:(k + 1) * P], identity[:, :])
                last.then_inc(dst_turned, 1)
            pe.wait_ge(rest_ready, 1)
            pe.transpose(turned_bank[0:1, 1, 0:P], rest_min[:, :], identity[:, :])
            pe.transpose(turned_bank[0:1, 1, P:P + tiles], above_min[0:tiles, :], identity[0:tiles, 0:tiles]).then_inc(rest_turned, 1)

            def sums(bank_slot, slot):
                for c in range(CHUNKS):
                    last = pe.matmul(sums_bank[:, bank_slot, 0:P], rows[:, slot, c, :], hot[:, slot, c, :],
                                     start=(c == 0), stop=(c == CHUNKS - 1))
                return last

            def turn(k, t):
                for j in range(SLOTS):
                    pe.wait_ge(hot_ready[j], t + (k * turns + 1))
                    pe.wait_ge(added[j - 2], t + (k * turns + (j >= 2)))
                    pe.wait_ge(rows_landed[j], t * (16 * CHUNKS) + (k * turns + 1) * 16 * CHUNKS)
                    sums(j % 2, j).then_inc(summed[j], 1)
                    if k == 0:
                        i = j % 2
                        pe.wait_ge(degree_hot[i], t * (SLOTS // 2) + (j // 2 + 1))
                        for c in range(CHUNKS):
                            last = pe.matmul(degree, hot_row[:, i, c, :], hot_block[:, i, c, :],
                                             start=False, stop=False, skip_group_check=True)
                        last.then_inc(degree_summed[i], 1)

            def own_step(s, nth, finished):
                pe.wait_ge(own_h, nth + 1)
                pe.wait_ge(own_added, nth)
                for b in range(FIVE):
                    last = pe.transpose(own[:, b * P:(b + 1) * P], fresh[:, b * P:(b + 1) * P], identity[:, :])
                last.then_inc(own_turned, 1)
                pe.wait_ge(own_staged, nth + 1)
                pe.matmul(own[:, 0:4 * P], w_own[:, :], staged[:, 0:4 * P], start=True, stop=True)
                pe.matmul(own[:, 4 * P:batch], w_own[:, :], staged[:, 4 * P:batch], start=True, stop=True).then_inc(own_summed, 1)

            def finish(k, s, after, owned):
                if k == 0:
                    pe.wait_ge(degree_read, s + 1)
                pe.wait_ge(stage_ready, s + (k * total + 1))
                pe.wait_ge(turned_used, s + k * total)
                for b in range(FIVE):
                    last = pe.transpose(turned[:, b * P:(b + 1) * P], staged[:, b * P:(b + 1) * P], identity[:, :])
                last.then_inc(stage_turned, 1)

            def outside(k):
                pe.wait_ge(added[SLOTS - 1], (k + 1) * turns)
                with pe.Fori(0, groups) as g:
                    landed, = ready_early(pe, g * (16 * CHUNKS) + (k * groups + 1) * 16 * CHUNKS)
                    pe.wait_ge(added[0], (k + 1) * turns)
                    pe.wait_ge(rest_landed, landed)
                    with pe.Fori(0, blocks) as w:
                        pe.wait_ge(rest_hot, g * blocks + w + (k * rest_turns + 1))
                        pe.wait_ge(rest_added, g * blocks + w + k * rest_turns)
                        sums(0, 0).then_inc(rest_summed, 1)

            for k in range(1 + HOPS):
                one_pass(pe, k, turn, own_step, finish, outside)

        @block.vector
        def _(dve):
            chain = Steps(dve, step)
            done = chain.then_wait
            dve.memset(state[:, whole * P:padded], 0.0).then_inc(padded_x, 1)
            for raw, value in ((raw_src, 0), (raw_type, 0), (raw_dst, FAR)):
                dve.memset(raw[:, (tiles - 1) * P:tiles * P], value).then_inc(padded_edges, 1)
            dve.wait_ge(iota_made, 1)
            dve.tensor_copy(count_up, iota[:, :]).then_inc(count_made, 1)
            dve.wait_ge(weights_turned, 1)
            dve.tensor_copy(w_types[:, :], turned_bank[:, 0, 0:2 * P])
            dve.tensor_copy(w_own[:, :], turned_bank[:, 0, 2 * P:3 * P]).then_inc(weights_copied, 1)
            for n in range(LOADS):
                dve.wait_ge(x_in[n], 16 * ((n * load < whole) + (tail > 0 and n * load <= whole < (n + 1) * load)))
                with dve.Fori(0, load // FIVE) as t:
                    for b in range(FIVE):
                        at = t * FIVE + (n * load + b)
                        last = dve.bn_stats(bn[:, ds(at, 1), :], state[:, ds(at * P, P)])
                    last.then_inc(x_measured, 1)
            dve.wait_ge(x_measured, blocks // FIVE)

            def variances(n, into, ready, wait):
                dve.tensor_tensor(means[:, 0:n], bn[:, 0:n, 1], bn[:, 0:n, 4], ALU.add)
                dve.tensor_tensor(squares[:, 0:n], bn[:, 0:n, 2], bn[:, 0:n, 5], ALU.add)
                wait(dve.tensor_tensor(skew[:, 0:n], bn[:, 0:n, 1], bn[:, 0:n, 4], ALU.subtract))
                wait(dve.scalar_tensor_tensor(out=skew[:, 0:n], in0=skew[:, 0:n], scalar=0.25, in1=skew[:, 0:n],
                                              op0=ALU.mult, op1=ALU.mult))
                wait(dve.scalar_tensor_tensor(out=squares[:, 0:n], in0=squares[:, 0:n], scalar=1.0 / P, in1=skew[:, 0:n],
                                              op0=ALU.mult, op1=ALU.add))
                dve.tensor_scalar(into, squares[:, 0:n], EPS, None, ALU.add).then_inc(ready, 1)

            variances(blocks, spread[:, :], variance_ready, done)
            dve.wait_ge(spread_ready, 1)
            done(dve.reciprocal(rstd[:, :], spread[:, :]))
            dve.scalar_tensor_tensor(out=shift[:, :], in0=means[:, :], scalar=-0.5, in1=rstd[:, :],
                                     op0=ALU.mult, op1=ALU.mult).then_inc(norm_ready, 1)
            biases = b_types[:, :].unsqueeze(1).to_broadcast([P, PAIR, 2 * P])
            with dve.Fori(0, pair_turns) as t:
                for i in range(2):
                    dve.wait_ge(message_stored[i], t * 32)
                    dve.wait_ge(typed_summed[i], t + 1)
                    dve.tensor_tensor(in_blocks(messages[i], PAIR), in_blocks(sums_bank[:, i, :], PAIR), biases, ALU.add
                                      ).then_inc(message_ready[i], 1)

            dve.wait_ge(dst_ready, 1)
            dve.tensor_reduce(chunk_min[:, :], raw_dst.bitcast(F32).rearrange("p (k e) -> p k e", k=tiles), AX_X, ALU.min
                              ).then_inc(min_ready, 1)
            dve.wait_ge(min_turned, 1)
            done(dve.tensor_reduce(group_min[0:tiles, :], turned_bank[0:tiles, 0, 0:P].rearrange("k (g c) -> k g c", c=CHUNKS),
                                   AX_X, ALU.min))
            dve.tensor_scalar(group_base[0:tiles, :], group_min[0:tiles, :], float(n_nodes - 1), 0.0, ALU.min, ALU.max
                              ).then_inc(base_made, 1)
            for n in range(0, tiles, 4):
                columns = slice(n * P, min(n + 4, tiles) * P)
                size = columns.stop - columns.start
                dve.wait_ge(dst_turned, n // 4 + 1)
                dve.tensor_copy(local[:, columns], own_bank[:, n // 4 % 2, 0:size])
                dve.tensor_copy(dst_row[:, columns], own_bank[:, n // 4 % 2, 0:size]).then_inc(dst_copied, 1)
            dve.wait_ge(dst_copied, -(-tiles // 4))
            done(dve.tensor_copy(rest[:, :], local[:, :]))
            dve.wait_ge(base_in, 32)
            by_group = local[:, :].rearrange("p (g c) -> p g c", c=CHUNKS)
            bases = base_all[:, :].unsqueeze(2).to_broadcast([P, groups, CHUNKS])
            done(dve.tensor_tensor(by_group, by_group, bases, ALU.subtract))
            inside = dst_block[:, :].bitcast(F32)
            done(dve.tensor_scalar(inside, local[:, :], float(P), float(FAR), ALU.is_lt, ALU.mult))
            done(dve.tensor_tensor(rest[:, :], rest[:, :], inside, ALU.max))
            dve.wait_ge(line_made, 1)
            dve.wait_ge(base_made, 1)
            done(dve.tensor_tensor(above[0:tiles, :], group_base[0:tiles, :], line[0:tiles, :], ALU.add))
            dve.tensor_reduce(above_min[0:tiles, :], above[0:tiles, :], AX_X, ALU.min)
            dve.tensor_reduce(rest_min[:, :], rest[:, :], AX_X, ALU.min).then_inc(rest_ready, 1)
            dve.tensor_single_scalar(dst_block[:, :], dst_row[:, :], 7, ALU.logical_shift_right).then_inc(step, 1)
            dve.tensor_single_scalar(dst_row[:, :], dst_row[:, :], P - 1, ALU.bitwise_and).then_inc(step, 1)
            chain.done += 2
            dve.wait_ge(rest_turned, 1)
            dve.tensor_reduce(checks[0:1, 0:1], turned_bank[0:1, 1, 0:P], AX_X, ALU.min)
            done(dve.tensor_reduce(checks[0:1, 1:2], turned_bank[0:1, 1, P:P + tiles], AX_X, ALU.min))
            dve.tensor_scalar(checks[0:1, 2:3], checks[0:1, 0:1], float(n_nodes), None, ALU.is_lt)
            done(dve.tensor_scalar(checks[0:1, 3:4], checks[0:1, 1:2], 0.0, None, ALU.is_lt))
            dve.tensor_tensor(uneven[0:1, :], checks[0:1, 2:3], checks[0:1, 3:4], ALU.max).then_inc(prepared, 1)
            dve.wait_ge(zeroed, 3)
            dve.wait_ge(index_copied, tiles)

            batch_chain = Steps(dve, batch_step)
            batch_done = batch_chain.then_wait
            chained = 7

            def turn(k, t):
                for j in range(SLOTS):
                    group = t * SLOTS + j
                    base = dve.value_load(base_row[0:1, ds(group, 1)], min_val=0, max_val=n_nodes - 1)
                    dve.wait_ge(summed[j], t + k * turns)
                    dve.tensor_tensor(hot[:, j, :, :], counting(P), over_hot(local[:, ds(group * CHUNKS, CHUNKS)], P),
                                      ALU.is_equal).then_inc(hot_ready[j], 1)
                    if k == 0:
                        i = j % 2
                        dve.wait_ge(degree_summed[i], t * (SLOTS // 2) + j // 2)
                        dve.tensor_tensor(hot_row[:, i, :, :], counting(P),
                                          over_hot(dst_row[:, ds(group * CHUNKS, CHUNKS)], P), ALU.is_equal)
                        dve.tensor_tensor(hot_block[:, i, :, :], counting(blocks),
                                          over_hot(dst_block[:, ds(group * CHUNKS, CHUNKS)], blocks),
                                          ALU.is_equal).then_inc(degree_hot[i], 1)
                    dve.wait_ge(added[j - 1], t + (k * turns + (j > 0)))
                    dve.wait_ge(summed[j], t + (k * turns + 1))
                    into = acc[:, ds(base, P)]
                    dve.tensor_tensor(into, sums_bank[:, j % 2, 0:P], into, ALU.add).then_inc(added[j], 1)

            def own_step(s, nth, finished):
                part = acc[:, ds(s * batch, batch)]
                dve.wait_ge(own_summed, nth + 1)
                dve.wait_ge(own_added, nth)
                dve.scalar_tensor_tensor(out=part, in0=own, scalar=b_own[:, 0:1], in1=part, op0=ALU.add, op1=ALU.add
                                         ).then_inc(own_added, 1)
                dve.wait_ge(own_added, nth + 1)

            def finish(k, s, after, owned):
                part = state[:, ds(s * batch, batch)]
                nth = s + k * total
                if k == 0:
                    batch_chain.begin(s * chained)
                    for i in range(2):
                        dve.wait_ge(degree_summed[i], after * (SLOTS // 2))
                    batch_degree = degree[:, ds(s * FIVE, FIVE)]
                    dve.tensor_scalar(linked[:, :], batch_degree, 0.0, None, ALU.is_gt)
                    dve.tensor_scalar(batch_spread[:, 1, :], batch_degree, 1.0, None, ALU.max).then_inc(degree_read, 1)
                    dve.wait_ge(stage_turned, nth + 1)
                    dve.tensor_tensor(part, turned, part, ALU.add).then_inc(turned_used, 1)
                    dve.wait_ge(turned_used, nth + 1)
                    for b in range(FIVE):
                        last = dve.bn_stats(bn[:, b, :], state[:, ds((s * FIVE + b) * P, P)])
                    batch_done(last)
                    variances(FIVE, batch_spread[:, 0, :], batch_variance, batch_done)
                    dve.wait_ge(batch_root, nth + 1)
                    batch_done(dve.reciprocal(batch_rstd[:, :, :], batch_spread[:, :, :]))
                    dve.scalar_tensor_tensor(out=batch_shift[:, :], in0=means[:, 0:FIVE], scalar=-0.5, in1=batch_rstd[:, 0, :],
                                             op0=ALU.mult, op1=ALU.mult).then_inc(batch_norm, 1)
                    factors = inv[:, ds(s * FIVE, FIVE)]
                    batch_done(dve.tensor_tensor(factors, batch_rstd[:, 1, :], linked[:, :], ALU.mult))
                    batch_done(dve.tensor_scalar(inv_third[:, ds(s * FIVE, FIVE)], factors, 1.0 / (HOPS + 1), None, ALU.mult))
                    assert batch_chain.done == chained
                    dve.wait_ge(scaled_stored, nth * 16)
                    dve.wait_ge(fresh_ready, nth + 1)
                    dve.tensor_tensor(in_blocks(scaled[:, :]), in_blocks(fresh[:, :]), over_features(factors), ALU.mult
                                      ).then_inc(scaled_ready, 1)
                    dve.scalar_tensor_tensor(out=part, in0=fresh[:, :], scalar=1.0 / (HOPS + 1), in1=part,
                                             op0=ALU.mult, op1=ALU.add).then_inc(fresh_used, 1)
                elif k < HOPS:
                    factors = over_features(inv[:, ds(s * FIVE, FIVE)])
                    dve.wait_ge(fresh_used, nth)
                    dve.wait_ge(stage_turned, nth + 1)
                    dve.tensor_tensor(in_blocks(fresh[:, :]), in_blocks(turned), factors, ALU.mult).then_inc(turned_used, 1)
                    dve.wait_ge(turned_used, nth + 1)
                    dve.wait_ge(scaled_stored, nth * 16)
                    dve.tensor_tensor(in_blocks(scaled[:, :]), in_blocks(fresh[:, :]), factors, ALU.mult).then_inc(scaled_ready, 1)
                    dve.scalar_tensor_tensor(out=part, in0=fresh[:, :], scalar=1.0 / (HOPS + 1), in1=part,
                                             op0=ALU.mult, op1=ALU.add).then_inc(fresh_used, 1)
                else:
                    dve.wait_ge(fresh_used, HOPS * total)
                    dve.wait_ge(scaled_ready, nth)
                    dve.wait_ge(stage_turned, nth + 1)
                    dve.tensor_tensor(in_blocks(fresh[:, :]), in_blocks(turned),
                                      over_features(inv_third[:, ds(s * FIVE, FIVE)]), ALU.mult).then_inc(turned_used, 1)
                    dve.wait_ge(turned_used, nth + 1)
                    dve.wait_ge(scaled_stored, nth * 16)
                    dve.tensor_tensor(scaled[:, :], fresh[:, :], part, ALU.add).then_inc(scaled_ready, 1)

            def outside(k):
                dve.wait_ge(added[SLOTS - 1], (k + 1) * turns)
                with dve.Fori(0, groups) as g:
                    steps = g * (blocks + 1) + k * groups * (blocks + 1)
                    dve.wait_ge(rest_hot, g * blocks + k * rest_turns)
                    dve.wait_ge(rest_step, steps)
                    dve.tensor_copy(window[:, :], rest[:, ds(g * CHUNKS, CHUNKS)]).then_inc(rest_step, 1)
                    with dve.Fori(0, blocks) as w:
                        dve.wait_ge(rest_step, steps + w + 1)
                        dve.wait_ge(rest_summed, g * blocks + w + k * rest_turns)
                        dve.tensor_tensor(hot[:, 0, :, :], counting(P), over_hot(window[:, :], P),
                                          ALU.is_equal).then_inc(rest_hot, 1)
                        dve.wait_ge(rest_hot, g * blocks + w + (k * rest_turns + 1))
                        dve.tensor_scalar(window[:, :], window[:, :], float(P), None, ALU.subtract).then_inc(rest_step, 1)
                        dve.wait_ge(rest_added, g * blocks + w + k * rest_turns)
                        dve.wait_ge(rest_summed, g * blocks + w + (k * rest_turns + 1))
                        into = acc[:, ds(w * P, P)]
                        dve.tensor_tensor(into, sums_bank[:, 0, 0:P], into, ALU.add).then_inc(rest_added, 1)
                dve.wait_ge(rest_added, (k + 1) * rest_turns)

            for k in range(1 + HOPS):
                dve.wait_ge(acc_cleared, k * total)
                one_pass(dve, k, turn, own_step, finish, outside)


_INS = ["x", "src", "dst", "edge_type_2", "L0_gnn_W_data", "L0_gnn_b_data", "L0_gnn_W_control",
        "L0_gnn_b_control", "L0_gnn_W_self", "L0_gnn_b_self"]


def kernel(**inputs):
    import numpy as _np
    import concourse.bacc as _bacc
    from concourse.bass_utils import run_bass_kernel_spmd as _run

    nc = _bacc.Bacc("TRN2", target_bir_lowering=False, num_devices=1)
    arrays, args = {}, []
    for name in _INS:
        a = _np.ascontiguousarray(inputs[name])
        arrays[f"in_{name}"] = a
        args.append(nc.dram_tensor(f"in_{name}", a.shape, mybir.dt.from_np(a.dtype), kind="ExternalInput").ap())
    out = nc.dram_tensor("out", arrays["in_x"].shape, F32, kind="ExternalOutput").ap()
    gnn_kernel(nc, *args, out)
    r = _run(nc, [arrays], core_ids=[0])
    return r.results[0]["out"]
```

```python
from contextlib import ExitStack

import concourse.bass as bass
from concourse import mybir

P = 128
CHUNKS = 8
GROUP = CHUNKS * P
TILE_GROUPS = P // CHUNKS
SLOTS = 4
PAIR = 2
PAIRS = 4
FIVE = 5
LEAD = 2
AHEAD = 1
SPAN = 8
PARTS = ((0, 3), (3, 6), (6, 8))
BATCHES = len(PARTS)
LOADS = 5
MEASURED = 10
FAR = 1 << 20
EPS = 1e-5
HOPS = 2

F32 = mybir.dt.float32
BF16 = mybir.dt.bfloat16
I32 = mybir.dt.int32
ALU = mybir.AluOpType
ACT = mybir.ActivationFunctionType
AX_X = mybir.AxisListType.X
ds = bass.ds


class Steps:

    def __init__(self, engine, semaphore):
        self.engine, self.semaphore, self.start, self.done = engine, semaphore, 0, 0

    def begin(self, start):
        self.start, self.done = start, 0

    def then_wait(self, instruction):
        instruction.then_inc(self.semaphore, 1)
        self.done += 1
        self.engine.wait_ge(self.semaphore, self.start + self.done)


def ready_early(engine, *values):
    for value in values:
        engine.compute_val(value)
    return values


def gnn_kernel(nc, x, src, dst, edge_type, w_data, b_data, w_control, b_control, w_self, b_self, out):
    n_nodes, features = x.shape
    n_edges = src.shape[0]
    assert features == P

    batch = FIVE * P
    padded = -(-n_nodes // (2 * batch)) * 2 * batch
    blocks = padded // P
    whole = n_nodes // P
    tail = n_nodes - whole * P
    pair_turns = (blocks // PAIR - 1) // PAIRS
    last_pairs = blocks // PAIR - pair_turns * PAIRS
    total = blocks // FIVE
    load = blocks // LOADS
    assert n_nodes > padded - batch and blocks <= P and blocks % LOADS == 0 and load % MEASURED == 0

    tiles = -(-n_edges // (P * P))
    chunks = tiles * P
    groups = tiles * TILE_GROUPS
    turns = groups // SLOTS
    last_edge = (tiles - 1) * P * P
    full_rows = (n_edges - last_edge) // P
    odd_edges = n_edges - last_edge - full_rows * P

    whole_groups = (CHUNKS,) * SLOTS
    last_sizes = [max(1, min(CHUNKS, -(-n_edges // P) - ((turns - 1) * SLOTS + j) * CHUNKS)) for j in range(SLOTS)]
    landed_each = [16 * ((turns - 1) * CHUNKS + size) for size in last_sizes]

    spans = (turns - LEAD - AHEAD) // SPAN
    assert AHEAD <= 1 and (LEAD + AHEAD) * SLOTS <= TILE_GROUPS
    late = list(range(spans * BATCHES, total))
    slope = BATCHES * batch // (SPAN * SLOTS)
    assert late and all((n + 1) * batch <= slope * SLOTS * after for n, (_, after) in enumerate(PARTS))

    typed_table = nc.dram_tensor("typed_table", (2 * padded, P), F32, kind="Internal").ap()
    tables = [typed_table] + [nc.dram_tensor(f"hop_table{n}", (padded, P), F32, kind="Internal").ap() for n in range(HOPS)]
    base_dram = nc.dram_tensor("base_dram", (1, groups), I32, kind="Internal").ap()

    with ExitStack() as ctx:
        def sbuf(name, shape, dtype=F32):
            return ctx.enter_context(nc.sbuf_tensor(name, [P, *shape], dtype))

        def semaphore(name):
            return ctx.enter_context(nc.semaphore(name))

        def semaphores(name, n):
            return [semaphore(f"{name}{i}") for i in range(n)]

        state = sbuf("state", [padded])
        acc = sbuf("acc", [padded + P])
        index = sbuf("index", [2, chunks], I32)
        local = sbuf("local", [chunks])
        rest = sbuf("rest", [chunks])
        dst_block = sbuf("dst_block", [chunks], I32)
        dst_row = sbuf("dst_row", [chunks], I32)
        rows = sbuf("rows", [SLOTS, CHUNKS, P])
        hot = sbuf("hot", [SLOTS, CHUNKS, P])
        ring_index = sbuf("ring_index", [SLOTS, CHUNKS], I32)
        hot_row = sbuf("hot_row", [2, CHUNKS, P], BF16)
        hot_block = sbuf("hot_block", [2, CHUNKS, blocks], BF16)
        staged = sbuf("staged", [batch])
        fresh = sbuf("fresh", [batch])
        scaled = sbuf("scaled", [batch])
        zeros = sbuf("zeros", [P])
        iota = sbuf("iota", [P], I32)
        identity = sbuf("identity", [P])
        weights = sbuf("weights", [3, P])
        w_types = sbuf("w_types", [2 * P])
        w_own = sbuf("w_own", [P])
        b_types = sbuf("b_types", [2 * P])
        b_own = sbuf("b_own", [1])
        bn = sbuf("bn", [blocks, 6])
        means = sbuf("means", [blocks])
        skew = sbuf("skew", [blocks])
        squares = sbuf("squares", [blocks])
        spread = sbuf("spread", [blocks])
        rstd = sbuf("rstd", [blocks])
        shift = sbuf("shift", [blocks])
        batch_spread = sbuf("batch_spread", [2, FIVE])
        batch_rstd = sbuf("batch_rstd", [2, FIVE])
        batch_shift = sbuf("batch_shift", [FIVE])
        linked = sbuf("linked", [FIVE])
        inv = sbuf("inv", [blocks])
        inv_third = sbuf("inv_third", [blocks])
        chunk_min = sbuf("chunk_min", [tiles])
        group_min = sbuf("group_min", [TILE_GROUPS])
        group_base = sbuf("group_base", [TILE_GROUPS], I32)
        line = sbuf("line", [TILE_GROUPS], I32)
        above = sbuf("above", [TILE_GROUPS])
        above_min = sbuf("above_min", [1])
        base_row = sbuf("base_row", [groups], I32)
        base_all = sbuf("base_all", [groups], I32)
        rest_min = sbuf("rest_min", [1])
        checks = sbuf("checks", [4])
        uneven = sbuf("uneven", [1], I32)
        window = sbuf("window", [CHUNKS])

        raw_src = hot[:, 0:2].rearrange("p s c f -> p (s c f)")[:, 0:chunks].bitcast(I32)
        raw_type = hot[:, 2:4].rearrange("p s c f -> p (s c f)")[:, 0:chunks].bitcast(I32)
        raw_dst = dst_block[:, :]
        flat = rows[:, :].rearrange("p s c f -> p (s c f)")

        def carve(start, size, n=2):
            return [flat[:, start + i * size:start + (i + 1) * size] for i in range(n)]

        normed = carve(0, PAIR * P)
        normed_t = carve(2 * PAIR * P, PAIR * P)
        messages = carve(4 * PAIR * P, 2 * PAIR * P, PAIRS)
        assert chunks <= 2 * GROUP

        def bank(name, n):
            return ctx.enter_context(nc.psum_tensor(name, [P, n, 512], F32))

        sums_bank = bank("sums_bank", 2)
        turned_bank = bank("turned_bank", 2)
        own_bank = bank("own_bank", 2)
        degree = bank("degree", 1)[:, 0, 0:blocks]
        count_up = bank("count_up", 1)[:, 0, 0:P]
        turned = turned_bank[:, :, :].rearrange("p a f -> p (a f)")[:, 0:batch]
        own = own_bank[:, :, :].rearrange("p a f -> p (a f)")[:, 0:batch]

        src_in = semaphore("src_in")
        type_in = semaphore("type_in")
        dst_in = semaphore("dst_in")
        weights_in = semaphore("weights_in")
        x_in = semaphores("x_in", LOADS)
        padded_edges = semaphore("padded_edges")
        padded_x = semaphore("padded_x")
        zeroed = semaphore("zeroed")
        iota_made = semaphore("iota_made")
        line_made = semaphore("line_made")
        count_made = semaphore("count_made")
        identity_made = semaphore("identity_made")
        weights_turned = semaphore("weights_turned")
        weights_copied = semaphore("weights_copied")
        pool_step = semaphore("pool_step")
        sources_ready = semaphore("sources_ready")
        dst_ready = semaphore("dst_ready")
        index_turned = semaphore("index_turned")
        index_copied = semaphore("index_copied")
        dst_turned = semaphore("dst_turned")
        dst_copied = semaphore("dst_copied")
        min_ready = semaphore("min_ready")
        min_turned = semaphore("min_turned")
        base_made = semaphore("base_made")
        base_stored = semaphore("base_stored")
        base_in = semaphore("base_in")
        rest_ready = semaphore("rest_ready")
        rest_turned = semaphore("rest_turned")
        prepared = semaphore("prepared")
        x_measured = semaphore("x_measured")
        variance_ready = semaphore("variance_ready")
        spread_ready = semaphore("spread_ready")
        norm_ready = semaphore("norm_ready")
        h_ready = semaphores("h_ready", 2)
        h_turned = semaphores("h_turned", 2)
        h_copied = semaphores("h_copied", 2)
        typed_summed = semaphores("typed_summed", 2)
        message_ready = semaphores("message_ready", PAIRS)
        message_stored = semaphores("message_stored", PAIRS)
        index_ready = semaphores("index_ready", SLOTS)
        rows_landed = semaphores("rows_landed", SLOTS)
        hot_ready = semaphores("hot_ready", SLOTS)
        summed = semaphores("summed", SLOTS)
        added = semaphores("added", SLOTS)
        degree_hot = semaphores("degree_hot", 2)
        degree_summed = semaphores("degree_summed", 2)
        degree_read = semaphore("degree_read")
        own_h = semaphore("own_h")
        own_turned = semaphore("own_turned")
        own_staged = semaphore("own_staged")
        own_summed = semaphore("own_summed")
        own_added = semaphore("own_added")
        stage_ready = semaphore("stage_ready")
        acc_cleared = semaphore("acc_cleared")
        stage_turned = semaphore("stage_turned")
        turned_used = semaphore("turned_used")
        batch_variance = semaphore("batch_variance")
        batch_root = semaphore("batch_root")
        batch_norm = semaphore("batch_norm")
        fresh_ready = semaphore("fresh_ready")
        fresh_used = semaphore("fresh_used")
        scaled_ready = semaphore("scaled_ready")
        scaled_stored = semaphore("scaled_stored")
        step = semaphore("step")
        batch_step = semaphore("batch_step")
        rest_index = semaphore("rest_index")
        rest_landed = semaphore("rest_landed")
        rest_hot = semaphore("rest_hot")
        rest_summed = semaphore("rest_summed")
        rest_added = semaphore("rest_added")
        rest_step = semaphore("rest_step")

        rest_turns = groups * blocks

        def in_blocks(ap, n=FIVE):
            return ap.rearrange("p (b f) -> p b f", b=n)

        def over_features(ap, n=FIVE):
            return ap[:, 0:n].unsqueeze(2).to_broadcast([P, n, P])

        def held(s):
            return min(FIVE, -(-n_nodes // P) - s * FIVE) if isinstance(s, int) else FIVE

        def over_hot(ap, columns):
            return ap.unsqueeze(2).to_broadcast([P, CHUNKS, columns])

        def counting(columns):
            return count_up[:, 0:columns].unsqueeze(1).to_broadcast([P, CHUNKS, columns])

        def table_rows(table, first, n):
            return table[ds(first, n * P), :].rearrange("(b p) f -> p b f", p=P)

        def one_pass(engine, k, turn, own_step, finish, outside, ahead=0):
            lead = LEAD + ahead
            with engine.Fori(0, lead) as t:
                turn(k, t)
            if k == 0:
                for nth, s in enumerate(late):
                    own_step(s, nth, 0)
                engine.wait_ge(prepared, 1)
            flag = engine.value_load(uneven[0:1, 0:1], min_val=0, max_val=1)
            with engine.If(flag > 0):
                if k == 0:
                    with engine.Fori(0, spans * BATCHES) as s:
                        own_step(s, s + len(late), 0)
                with engine.Fori(lead, turns - 1) as t:
                    turn(k, t)
                turn(k, turns - 1, last_sizes)
                outside(k)
                with engine.Fori(0, total) as s:
                    finish(k, s, turns, total)
                engine.nop()
            with engine.Else():
                with engine.Fori(0, spans) as q:
                    for r, (start, end) in enumerate(PARTS):
                        with engine.Fori(start, end) as u:
                            turn(k, q * SPAN + u + lead)
                        if k == 0:
                            own_step(q * BATCHES + r, q * BATCHES + (r + len(late)), q * BATCHES + r)
                        finish(k, q * BATCHES + r, q * SPAN + (LEAD + end), q * BATCHES + (r + 1 + len(late)))
                if lead + spans * SPAN < turns - 1:
                    with engine.Fori(lead + spans * SPAN, turns - 1) as t:
                        turn(k, t)
                if ahead:
                    turn(k, turns - 1, last_sizes)
                for s in late[:-1]:
                    finish(k, s, turns - 1, total)
                if not ahead:
                    turn(k, turns - 1, last_sizes)
                finish(k, late[-1], turns, total)
                engine.nop()

        def pair_steps(engine, first, second):
            first(0, 0)
            with engine.Fori(0, pair_turns) as t:
                for i in range(PAIRS):
                    first(*((t, i + 1) if i + 1 < PAIRS else (t + 1, 0)))
                    second(t, i)
            for i in range(last_pairs):
                if i + 1 < last_pairs:
                    first(pair_turns, i + 1)
                second(pair_turns, i)

        def earlier(t, i):
            return t * (PAIRS // 2) + i // 2

        def nothing(*_):
            pass

        block = ctx.enter_context(nc.Block())

        @block.sync
        def _(sp):
            def edges(raw, array, landed):
                by_tile = raw.rearrange("p (k e) -> p k e", k=tiles)
                if tiles > 1:
                    sp.dma_start(by_tile[:, 0:tiles - 1, :],
                                 array[0:last_edge].rearrange("(k p e) -> p k e", p=P, e=P)).then_inc(landed, 16)
                if full_rows:
                    sp.dma_start(by_tile[0:full_rows, tiles - 1, :],
                                 array[last_edge:last_edge + full_rows * P].rearrange("(p e) -> p e", e=P)
                                 ).then_inc(landed, 16)
                if odd_edges:
                    sp.dma_start(by_tile[full_rows:full_rows + 1, tiles - 1, 0:odd_edges],
                                 array[n_edges - odd_edges:n_edges].rearrange("(p e) -> p e", p=1)
                                 ).then_inc(landed, 16)

            def nodes(n):
                first, end = n * load, min((n + 1) * load, whole)
                if end > first:
                    sp.dma_start(in_blocks(state[:, first * P:end * P], end - first),
                                 x[first * P:end * P, :].rearrange("(b p) f -> p b f", p=P)).then_inc(x_in[n], 16)
                if tail and n * load <= whole < (n + 1) * load:
                    sp.dma_start(state[0:tail, whole * P:(whole + 1) * P], x[whole * P:n_nodes, :]).then_inc(x_in[n], 16)

            sp.wait_ge(padded_x, 1)
            for n in range(LOADS):
                nodes(n)
            sp.wait_ge(padded_edges, 3)
            edges(raw_src, src, src_in)
            edges(raw_type, edge_type, type_in)
            edges(raw_dst, dst, dst_in)
            both_types = typed_table.rearrange("(b p k) f -> p b (k f)", p=P, k=2)

            def store_messages(t, i):
                sp.wait_ge(message_ready[i], t + 1)
                sp.dma_start(both_types[:, ds((t * PAIRS + i) * PAIR, PAIR), :], in_blocks(messages[i], PAIR)
                             ).then_inc(message_stored[i], 16)

            with sp.Fori(0, pair_turns) as t:
                for i in range(PAIRS):
                    store_messages(t, i)
            for i in range(last_pairs):
                store_messages(pair_turns, i)
            sp.wait_ge(base_made, 1)
            sp.dma_start(base_dram.rearrange("a (k g) -> (a k) g", k=tiles), group_base[0:tiles, :]).then_inc(base_stored, 16)
            sp.wait_ge(base_stored, 16)
            sp.dma_start(base_all[:, :], base_dram[0, :].partition_broadcast(P)).then_inc(base_in, 16)
            sp.dma_start(base_row[0:1, :], base_dram).then_inc(base_in, 16)
            for k in range(HOPS):
                with sp.Fori(0, total) as s:
                    sp.wait_ge(scaled_ready, s + (k * total + 1))
                    sp.dma_start(table_rows(tables[k + 1], s * batch, FIVE), in_blocks(scaled[:, :])).then_inc(scaled_stored, 16)
            full = n_nodes // batch
            with sp.Fori(0, full) as s:
                sp.wait_ge(scaled_ready, s + (HOPS * total + 1))
                sp.dma_start(out[ds(s * batch, batch), :].rearrange("(b p) f -> p b f", p=P), in_blocks(scaled[:, :])
                             ).then_inc(scaled_stored, 16)
            stored = HOPS * total + full
            if n_nodes % batch:
                sp.wait_ge(scaled_ready, stored + 1)
                n = whole - full * FIVE
                if n:
                    sp.dma_start(out[full * batch:whole * P, :].rearrange("(b p) f -> p b f", p=P),
                                 in_blocks(scaled[:, :])[:, 0:n, :]).then_inc(scaled_stored, 16)
                    stored += 1
                if tail:
                    sp.dma_start(out[whole * P:n_nodes, :], in_blocks(scaled[:, :])[0:tail, n, :]).then_inc(scaled_stored, 16)
                    stored += 1
            sp.wait_ge(scaled_stored, 16 * stored)

        @block.gpsimd
        def _(pool):
            pool.memset(zeros[:, :], 0.0).then_inc(zeroed, 1)
            pool.memset(identity[:, :], 0.0).then_inc(zeroed, 1)
            pool.iota(iota[:, :], pattern=[[1, P]], base=0, channel_multiplier=0).then_inc(iota_made, 1)
            pool.iota(line[:, :], pattern=[[-slope, TILE_GROUPS]], base=slope * SLOTS * LEAD,
                      channel_multiplier=-slope * TILE_GROUPS).then_inc(line_made, 1)
            pool.wait_ge(line_made, 1)
            pool.affine_select(out=line[:, :], in_=line[:, :], compare_op=ALU.is_ge, fill=-(total - 1) * batch,
                               base=(turns - 1) * SLOTS - 1, pattern=[[-1, TILE_GROUPS]], channel_multiplier=-TILE_GROUPS
                               ).then_inc(line_made, 1)
            pool.wait_ge(zeroed, 2)
            pool.affine_select(out=identity[:, :], in_=identity[:, :], compare_op=ALU.not_equal, fill=1.0,
                               base=0, pattern=[[-1, P]], channel_multiplier=1).then_inc(identity_made, 1)
            pool.memset(acc[:, :], 0.0).then_inc(zeroed, 1)
            arrivals = 16 * ((tiles > 1) + (full_rows > 0) + (odd_edges > 0))
            src_f, type_f, dst_f = (raw.bitcast(F32) for raw in (raw_src, raw_type, raw_dst))
            pool.wait_ge(src_in, arrivals)
            pool.tensor_copy(src_f, raw_src).then_inc(pool_step, 1)
            pool.wait_ge(type_in, arrivals)
            pool.tensor_copy(type_f, raw_type).then_inc(pool_step, 1)
            pool.wait_ge(pool_step, 2)
            pool.tensor_scalar(type_f, type_f, 0.0, None, ALU.is_equal).then_inc(pool_step, 1)
            pool.wait_ge(pool_step, 3)
            pool.tensor_tensor(type_f, type_f, src_f, ALU.add).then_inc(pool_step, 1)
            pool.wait_ge(pool_step, 4)
            pool.tensor_tensor(type_f, type_f, src_f, ALU.add).then_inc(sources_ready, 1)
            pool.wait_ge(dst_in, arrivals)
            pool.tensor_copy(dst_f, raw_dst).then_inc(dst_ready, 1)

            def gather(table, landed, slot, size=CHUNKS):
                for c in range(size):
                    pool.indirect_dma_start(
                        out=rows[:, slot, c, :], out_offset=None, in_=table,
                        in_offset=bass.IndirectOffsetOnAxis(ap=ring_index[:, slot, c:c + 1], axis=0)).then_inc(landed, 16)

            def stored(k, i):
                return (message_stored[i], 16 * (pair_turns + (i < last_pairs))) if k == 0 else (scaled_stored, 16 * k * total)

            def turn(k, t, sizes=whole_groups):
                for j in range(SLOTS):
                    uses, before = t + (k * turns + 1), t + k * turns
                    ready_early(pool, uses, before)
                    pool.wait_ge(*stored(k, 0))
                    pool.wait_ge(index_ready[j], uses)
                    pool.wait_ge(summed[j], before)
                    gather(tables[k], rows_landed[j], j, sizes[j])

            def outside(k):
                pool.wait_ge(summed[0], (k + 1) * turns)
                with pool.Fori(0, groups) as g:
                    uses, before = ready_early(pool, g + (k * groups + 1), g * blocks + k * rest_turns)
                    pool.wait_ge(*stored(k, 0))
                    pool.wait_ge(rest_index, uses)
                    pool.wait_ge(rest_summed, before)
                    gather(tables[k], rest_landed, 0)

            for k in range(1 + HOPS):
                for i in range(1, PAIRS if k == 0 else 2):
                    pool.wait_ge(*stored(k, i))
                one_pass(pool, k, turn, nothing, nothing, outside)

        @block.scalar
        def _(act):
            for n, w in enumerate((w_control, w_data, w_self)):
                act.dma_start(weights[:, n, :], w).then_inc(weights_in, 16)
            act.dma_start(b_types[:, P:2 * P], b_data.partition_broadcast(P)).then_inc(weights_in, 16)
            act.dma_start(b_types[:, 0:P], b_control.partition_broadcast(P)).then_inc(weights_in, 16)
            act.dma_start(b_own[:, :], b_self.rearrange("(p a) -> p a", a=1)).then_inc(weights_in, 16)
            act.wait_ge(variance_ready, 1)
            act.activation(spread[:, :], spread[:, :], ACT.Sqrt).then_inc(spread_ready, 1)

            def normalise(into, block, scales, biases, n):
                values = state[:, ds(block * P, n * P)]
                for b in range(n):
                    last = act.activation(into[:, b * P:(b + 1) * P], values[:, b * P:(b + 1) * P], ACT.Relu,
                                          bias=biases[:, b:b + 1], scale=scales[:, b:b + 1])
                return last

            def normalise_x(into, block, n):
                return normalise(into, block, rstd[:, ds(block, n)], shift[:, ds(block, n)], n)

            def make_h(t, i):
                act.wait_ge(h_turned[i % 2], earlier(t, i))
                normalise_x(normed[i % 2], (t * PAIRS + i) * PAIR, PAIR).then_inc(h_ready[i % 2], 1)

            def copy_h(t, i):
                act.wait_ge(typed_summed[i % 2], earlier(t, i))
                act.wait_ge(h_turned[i % 2], earlier(t, i) + 1)
                act.copy(normed_t[i % 2], turned_bank[:, i % 2, 0:PAIR * P]).then_inc(h_copied[i % 2], 1)

            act.wait_ge(norm_ready, 1)
            pair_steps(act, make_h, copy_h)
            act.wait_ge(index_copied, 1)

            def turn(k, t, sizes=whole_groups):
                for j in range(SLOTS):
                    act.wait_ge(rows_landed[j], t * (16 * CHUNKS) + k * landed_each[j])
                    act.copy(ring_index[:, j, :], index[:, min(k, 1), ds((t * SLOTS + j) * CHUNKS, CHUNKS)]
                             ).then_inc(index_ready[j], 1)

            def own_step(s, nth, finished):
                act.wait_ge(own_turned, nth)
                act.wait_ge(fresh_used, finished)
                normalise_x(fresh, s * FIVE, FIVE).then_inc(own_h, 1)
                act.wait_ge(own_turned, nth + 1)
                act.wait_ge(own_summed, nth)
                act.copy(staged[:, :], own).then_inc(own_staged, 1)

            def finish(k, s, after, owned):
                part = acc[:, ds(s * batch, batch)]
                act.wait_ge(added[SLOTS - 1], after + k * turns)
                act.wait_ge(stage_turned, s + k * total)
                if k == 0:
                    act.wait_ge(own_added, owned)
                n = held(s)
                act.activation(staged[:, 0:n * P], part[:, 0:n * P], ACT.Relu if k == 0 else ACT.Copy).then_inc(stage_ready, 1)
                if k < HOPS:
                    act.wait_ge(stage_ready, s + (k * total + 1))
                    part = acc[:, ds(act.compute_val(s * batch), batch)]
                    act.copy(part, zeros[:, 0:1].to_broadcast([P, batch])).then_inc(acc_cleared, 1)
                if k == 0:
                    act.wait_ge(batch_variance, s + 1)
                    act.activation(batch_spread[:, :, :], batch_spread[:, :, :], ACT.Sqrt).then_inc(batch_root, 1)
                    act.wait_ge(norm_ready, 1)
                    act.wait_ge(batch_norm, s + 1)
                    act.wait_ge(fresh_used, s)
                    normalise(fresh, s * FIVE, batch_rstd[:, 0, :], batch_shift, n
                              ).then_inc(fresh_ready, 1)

            def outside(k):
                act.wait_ge(rows_landed[0], (k + 1) * landed_each[0])
                with act.Fori(0, groups) as g:
                    act.wait_ge(rest_landed, g * (16 * CHUNKS) + k * groups * 16 * CHUNKS)
                    act.copy(ring_index[:, 0, :], index[:, min(k, 1), ds(g * CHUNKS, CHUNKS)]).then_inc(rest_index, 1)
                act.wait_ge(rest_added, (k + 1) * rest_turns)

            for k in range(1 + HOPS):
                one_pass(act, k, turn, own_step, finish, outside, AHEAD)

        @block.tensor
        def _(pe):
            pe.wait_ge(identity_made, 1)
            pe.wait_ge(weights_in, 16 * 6)
            for n in range(3):
                last = pe.transpose(turned_bank[:, 0, n * P:(n + 1) * P], weights[:, n, :], identity[:, :])
            last.then_inc(weights_turned, 1)
            pe.matmul(degree, zeros[:, :], zeros[:, 0:blocks], start=True, stop=False, skip_group_check=True)
            def turn_h(t, i):
                pe.wait_ge(h_ready[i % 2], earlier(t, i) + 1)
                pe.wait_ge(h_copied[i % 2], earlier(t, i))
                for b in range(PAIR):
                    last = pe.transpose(turned_bank[:, i % 2, b * P:(b + 1) * P], normed[i % 2][:, b * P:(b + 1) * P], identity[:, :])
                last.then_inc(h_turned[i % 2], 1)

            def type_h(t, i):
                pe.wait_ge(h_copied[i % 2], earlier(t, i) + 1)
                if i >= 2:
                    pe.wait_ge(message_ready[i - 2], t + 1)
                else:
                    pe.wait_ge(message_ready[i + 2], t)
                for b in range(PAIR):
                    last = pe.matmul(sums_bank[:, i % 2, b * 2 * P:(b + 1) * 2 * P], normed_t[i % 2][:, b * P:(b + 1) * P],
                                     w_types[:, :], start=True, stop=True)
                last.then_inc(typed_summed[i % 2], 1)

            pe.wait_ge(weights_copied, 1)
            pair_steps(pe, turn_h, type_h)
            pe.wait_ge(sources_ready, 1)
            for k in range(tiles):
                if k >= 2:
                    pe.wait_ge(index_copied, k - 1)
                for n, raw in enumerate((raw_type, raw_src)):
                    last = pe.transpose(own_bank[:, k % 2, n * P:(n + 1) * P], raw.bitcast(F32)[:, k * P:(k + 1) * P], identity[:, :])
                last.then_inc(index_turned, 1)
            pe.wait_ge(index_copied, tiles)
            pe.wait_ge(min_ready, 1)
            pe.transpose(turned_bank[0:tiles, 0, 0:P], chunk_min[:, :], identity[:, :]).then_inc(min_turned, 1)
            for n in range(0, tiles, 4):
                if n >= 8:
                    pe.wait_ge(dst_copied, n // 4 - 1)
                for k in range(n, min(n + 4, tiles)):
                    last = pe.transpose(own_bank[:, n // 4 % 2, (k - n) * P:(k - n + 1) * P],
                                        raw_dst.bitcast(F32)[:, k * P:(k + 1) * P], identity[:, :])
                last.then_inc(dst_turned, 1)
            pe.wait_ge(rest_ready, 1)
            pe.transpose(turned_bank[0:1, 1, 0:P], rest_min[:, :], identity[:, :])
            pe.transpose(turned_bank[0:1, 1, P:P + tiles], above_min[0:tiles, :], identity[0:tiles, 0:tiles]).then_inc(rest_turned, 1)

            def sums(bank_slot, slot, size=CHUNKS):
                for c in range(size):
                    last = pe.matmul(sums_bank[:, bank_slot, 0:P], rows[:, slot, c, :], hot[:, slot, c, :],
                                     start=(c == 0), stop=(c == size - 1))
                return last

            def turn(k, t, sizes=whole_groups):
                for j in range(SLOTS):
                    pe.wait_ge(hot_ready[j], t + (k * turns + 1))
                    pe.wait_ge(added[j - 2], t + (k * turns + (j >= 2)))
                    pe.wait_ge(rows_landed[j], t * (16 * CHUNKS) + (k * landed_each[j] + 16 * sizes[j]))
                    sums(j % 2, j, sizes[j]).then_inc(summed[j], 1)
                    if k == 0:
                        i = j % 2
                        pe.wait_ge(degree_hot[i], t * (SLOTS // 2) + (j // 2 + 1))
                        for c in range(sizes[j]):
                            last = pe.matmul(degree, hot_row[:, i, c, :], hot_block[:, i, c, :],
                                             start=False, stop=False, skip_group_check=True)
                        last.then_inc(degree_summed[i], 1)

            def own_step(s, nth, finished):
                pe.wait_ge(own_h, nth + 1)
                pe.wait_ge(own_added, nth)
                for b in range(FIVE):
                    last = pe.transpose(own[:, b * P:(b + 1) * P], fresh[:, b * P:(b + 1) * P], identity[:, :])
                last.then_inc(own_turned, 1)
                pe.wait_ge(own_staged, nth + 1)
                pe.matmul(own[:, 0:4 * P], w_own[:, :], staged[:, 0:4 * P], start=True, stop=True)
                pe.matmul(own[:, 4 * P:batch], w_own[:, :], staged[:, 4 * P:batch], start=True, stop=True).then_inc(own_summed, 1)

            def finish(k, s, after, owned):
                if k == 0:
                    pe.wait_ge(degree_read, s + 1)
                pe.wait_ge(stage_ready, s + (k * total + 1))
                pe.wait_ge(turned_used, s + k * total)
                for b in range(held(s)):
                    last = pe.transpose(turned[:, b * P:(b + 1) * P], staged[:, b * P:(b + 1) * P], identity[:, :])
                last.then_inc(stage_turned, 1)

            def outside(k):
                pe.wait_ge(added[SLOTS - 1], (k + 1) * turns)
                with pe.Fori(0, groups) as g:
                    landed, = ready_early(pe, g * (16 * CHUNKS) + (k * groups + 1) * 16 * CHUNKS)
                    pe.wait_ge(added[0], (k + 1) * turns)
                    pe.wait_ge(rest_landed, landed)
                    with pe.Fori(0, blocks) as w:
                        pe.wait_ge(rest_hot, g * blocks + w + (k * rest_turns + 1))
                        pe.wait_ge(rest_added, g * blocks + w + k * rest_turns)
                        sums(0, 0).then_inc(rest_summed, 1)

            for k in range(1 + HOPS):
                one_pass(pe, k, turn, own_step, finish, outside)

        @block.vector
        def _(dve):
            chain = Steps(dve, step)
            done = chain.then_wait
            dve.memset(state[:, whole * P:padded], 0.0).then_inc(padded_x, 1)
            for raw, value in ((raw_src, 0), (raw_type, 0), (raw_dst, FAR)):
                dve.memset(raw[:, (tiles - 1) * P:tiles * P], value).then_inc(padded_edges, 1)
            dve.wait_ge(iota_made, 1)
            dve.tensor_copy(count_up, iota[:, :]).then_inc(count_made, 1)
            def measure(statistics, values, n):
                for b in range(n):
                    last = dve.bn_stats(statistics[:, b, :], values[:, b * P:(b + 1) * P])
                return last

            for n in range(LOADS):
                dve.wait_ge(x_in[n], 16 * ((n * load < whole) + (tail > 0 and n * load <= whole < (n + 1) * load)))
                with dve.Fori(0, load // MEASURED) as t:
                    first = t * MEASURED + n * load
                    measure(bn[:, ds(first, MEASURED), :], state[:, ds(first * P, MEASURED * P)], MEASURED).then_inc(x_measured, 1)
            dve.wait_ge(weights_turned, 1)
            dve.tensor_copy(w_types[:, :], turned_bank[:, 0, 0:2 * P])
            dve.tensor_copy(w_own[:, :], turned_bank[:, 0, 2 * P:3 * P]).then_inc(weights_copied, 1)
            dve.wait_ge(x_measured, blocks // MEASURED)

            def variances(n, into, ready, wait):
                dve.tensor_tensor(means[:, 0:n], bn[:, 0:n, 1], bn[:, 0:n, 4], ALU.add)
                dve.tensor_tensor(squares[:, 0:n], bn[:, 0:n, 2], bn[:, 0:n, 5], ALU.add)
                wait(dve.tensor_tensor(skew[:, 0:n], bn[:, 0:n, 1], bn[:, 0:n, 4], ALU.subtract))
                wait(dve.scalar_tensor_tensor(out=skew[:, 0:n], in0=skew[:, 0:n], scalar=0.25, in1=skew[:, 0:n],
                                              op0=ALU.mult, op1=ALU.mult))
                wait(dve.scalar_tensor_tensor(out=squares[:, 0:n], in0=squares[:, 0:n], scalar=1.0 / P, in1=skew[:, 0:n],
                                              op0=ALU.mult, op1=ALU.add))
                dve.tensor_scalar(into, squares[:, 0:n], EPS, None, ALU.add).then_inc(ready, 1)

            variances(blocks, spread[:, :], variance_ready, done)
            dve.wait_ge(spread_ready, 1)
            done(dve.reciprocal(rstd[:, :], spread[:, :]))
            dve.scalar_tensor_tensor(out=shift[:, :], in0=means[:, :], scalar=-0.5, in1=rstd[:, :],
                                     op0=ALU.mult, op1=ALU.mult).then_inc(norm_ready, 1)
            biases = b_types[:, :].unsqueeze(1).to_broadcast([P, PAIR, 2 * P])

            def add_biases(t, i):
                dve.wait_ge(message_stored[i], t * 16)
                dve.wait_ge(typed_summed[i % 2], earlier(t, i) + 1)
                dve.tensor_tensor(in_blocks(messages[i], PAIR), in_blocks(sums_bank[:, i % 2, :], PAIR), biases, ALU.add
                                  ).then_inc(message_ready[i], 1)

            with dve.Fori(0, pair_turns) as t:
                for i in range(PAIRS):
                    add_biases(t, i)
            for i in range(last_pairs):
                add_biases(pair_turns, i)
            for k in range(tiles):
                dve.wait_ge(index_turned, k + 1)
                dve.tensor_copy(index[:, :, k * P:(k + 1) * P], own_bank[:, k % 2, 0:2 * P].rearrange("p (a c) -> p a c", a=2)
                                ).then_inc(index_copied, 1)
            dve.wait_ge(dst_ready, 1)
            dve.tensor_reduce(chunk_min[:, :], raw_dst.bitcast(F32).rearrange("p (k e) -> p k e", k=tiles), AX_X, ALU.min
                              ).then_inc(min_ready, 1)
            dve.wait_ge(min_turned, 1)
            done(dve.tensor_reduce(group_min[0:tiles, :], turned_bank[0:tiles, 0, 0:P].rearrange("k (g c) -> k g c", c=CHUNKS),
                                   AX_X, ALU.min))
            dve.tensor_scalar(group_base[0:tiles, :], group_min[0:tiles, :], float(n_nodes - 1), 0.0, ALU.min, ALU.max
                              ).then_inc(base_made, 1)
            for n in range(0, tiles, 4):
                columns = slice(n * P, min(n + 4, tiles) * P)
                size = columns.stop - columns.start
                dve.wait_ge(dst_turned, n // 4 + 1)
                dve.tensor_copy(local[:, columns], own_bank[:, n // 4 % 2, 0:size])
                dve.tensor_copy(dst_row[:, columns], own_bank[:, n // 4 % 2, 0:size]).then_inc(dst_copied, 1)
            dve.wait_ge(dst_copied, -(-tiles // 4))
            done(dve.tensor_copy(rest[:, :], local[:, :]))
            dve.wait_ge(base_in, 32)
            by_group = local[:, :].rearrange("p (g c) -> p g c", c=CHUNKS)
            bases = base_all[:, :].unsqueeze(2).to_broadcast([P, groups, CHUNKS])
            done(dve.tensor_tensor(by_group, by_group, bases, ALU.subtract))
            inside = dst_block[:, :].bitcast(F32)
            done(dve.tensor_scalar(inside, local[:, :], float(P), float(FAR), ALU.is_lt, ALU.mult))
            done(dve.tensor_tensor(rest[:, :], rest[:, :], inside, ALU.max))
            dve.wait_ge(line_made, 2)
            dve.wait_ge(base_made, 1)
            done(dve.tensor_tensor(above[0:tiles, :], group_base[0:tiles, :], line[0:tiles, :], ALU.add))
            dve.tensor_reduce(above_min[0:tiles, :], above[0:tiles, :], AX_X, ALU.min)
            dve.tensor_reduce(rest_min[:, :], rest[:, :], AX_X, ALU.min).then_inc(rest_ready, 1)
            dve.tensor_single_scalar(dst_block[:, :], dst_row[:, :], 7, ALU.logical_shift_right).then_inc(step, 1)
            dve.tensor_single_scalar(dst_row[:, :], dst_row[:, :], P - 1, ALU.bitwise_and).then_inc(step, 1)
            chain.done += 2
            dve.wait_ge(rest_turned, 1)
            dve.tensor_reduce(checks[0:1, 0:1], turned_bank[0:1, 1, 0:P], AX_X, ALU.min)
            done(dve.tensor_reduce(checks[0:1, 1:2], turned_bank[0:1, 1, P:P + tiles], AX_X, ALU.min))
            dve.tensor_scalar(checks[0:1, 2:3], checks[0:1, 0:1], float(n_nodes), None, ALU.is_lt)
            done(dve.tensor_scalar(checks[0:1, 3:4], checks[0:1, 1:2], 0.0, None, ALU.is_lt))
            dve.tensor_tensor(uneven[0:1, :], checks[0:1, 2:3], checks[0:1, 3:4], ALU.max).then_inc(prepared, 1)
            dve.wait_ge(zeroed, 3)
            dve.wait_ge(index_copied, tiles)

            batch_chain = Steps(dve, batch_step)
            batch_done = batch_chain.then_wait
            chained = 7

            def turn(k, t, sizes=whole_groups):
                for j in range(SLOTS):
                    group = t * SLOTS + j
                    base = dve.value_load(base_row[0:1, ds(group, 1)], min_val=0, max_val=n_nodes - 1)
                    dve.wait_ge(summed[j], t + k * turns)
                    dve.tensor_tensor(hot[:, j, :, :], counting(P), over_hot(local[:, ds(group * CHUNKS, CHUNKS)], P),
                                      ALU.is_equal).then_inc(hot_ready[j], 1)
                    if k == 0:
                        i = j % 2
                        dve.wait_ge(degree_summed[i], t * (SLOTS // 2) + j // 2)
                        dve.tensor_tensor(hot_row[:, i, :, :], counting(P),
                                          over_hot(dst_row[:, ds(group * CHUNKS, CHUNKS)], P), ALU.is_equal)
                        dve.tensor_tensor(hot_block[:, i, :, :], counting(blocks),
                                          over_hot(dst_block[:, ds(group * CHUNKS, CHUNKS)], blocks),
                                          ALU.is_equal).then_inc(degree_hot[i], 1)
                    dve.wait_ge(added[j - 1], t + (k * turns + (j > 0)))
                    dve.wait_ge(summed[j], t + (k * turns + 1))
                    into = acc[:, ds(base, P)]
                    dve.tensor_tensor(into, sums_bank[:, j % 2, 0:P], into, ALU.add).then_inc(added[j], 1)

            def own_step(s, nth, finished):
                part = acc[:, ds(s * batch, batch)]
                dve.wait_ge(own_summed, nth + 1)
                dve.wait_ge(own_added, nth)
                dve.scalar_tensor_tensor(out=part, in0=own, scalar=b_own[:, 0:1], in1=part, op0=ALU.add, op1=ALU.add
                                         ).then_inc(own_added, 1)
                dve.wait_ge(own_added, nth + 1)

            def finish(k, s, after, owned):
                n = held(s)
                size = n * P
                part = state[:, ds(s * batch, batch)][:, 0:size]
                nth = s + k * total
                if k == 0:
                    batch_chain.begin(s * chained)
                    for i in range(2):
                        dve.wait_ge(degree_summed[i], after * (SLOTS // 2))
                    batch_degree = degree[:, ds(s * FIVE, FIVE)]
                    dve.tensor_scalar(linked[:, :], batch_degree, 0.0, None, ALU.is_gt)
                    dve.tensor_scalar(batch_spread[:, 1, :], batch_degree, 1.0, None, ALU.max).then_inc(degree_read, 1)
                    dve.wait_ge(stage_turned, nth + 1)
                    dve.tensor_tensor(part, turned[:, 0:size], part, ALU.add).then_inc(turned_used, 1)
                    dve.wait_ge(turned_used, nth + 1)
                    values = state[:, ds(dve.compute_val(s * batch), batch)]
                    batch_done(measure(bn, values, n))
                    variances(FIVE, batch_spread[:, 0, :], batch_variance, batch_done)
                    dve.wait_ge(batch_root, nth + 1)
                    batch_done(dve.reciprocal(batch_rstd[:, :, :], batch_spread[:, :, :]))
                    dve.scalar_tensor_tensor(out=batch_shift[:, :], in0=means[:, 0:FIVE], scalar=-0.5, in1=batch_rstd[:, 0, :],
                                             op0=ALU.mult, op1=ALU.mult).then_inc(batch_norm, 1)
                    factors = inv[:, ds(s * FIVE, FIVE)]
                    batch_done(dve.tensor_tensor(factors, batch_rstd[:, 1, :], linked[:, :], ALU.mult))
                    batch_done(dve.tensor_scalar(inv_third[:, ds(s * FIVE, FIVE)], factors, 1.0 / (HOPS + 1), None, ALU.mult))
                    assert batch_chain.done == chained
                    dve.wait_ge(scaled_stored, nth * 16)
                    dve.wait_ge(fresh_ready, nth + 1)
                    dve.tensor_tensor(in_blocks(scaled[:, 0:size], n), in_blocks(fresh[:, 0:size], n), over_features(factors, n), ALU.mult
                                      ).then_inc(scaled_ready, 1)
                    dve.scalar_tensor_tensor(out=part, in0=fresh[:, 0:size], scalar=1.0 / (HOPS + 1), in1=part,
                                             op0=ALU.mult, op1=ALU.add).then_inc(fresh_used, 1)
                elif k < HOPS:
                    factors = over_features(inv[:, ds(s * FIVE, FIVE)], n)
                    dve.wait_ge(fresh_used, nth)
                    dve.wait_ge(stage_turned, nth + 1)
                    dve.tensor_tensor(in_blocks(fresh[:, 0:size], n), in_blocks(turned[:, 0:size], n), factors, ALU.mult).then_inc(turned_used, 1)
                    dve.wait_ge(turned_used, nth + 1)
                    dve.wait_ge(scaled_stored, nth * 16)
                    dve.tensor_tensor(in_blocks(scaled[:, 0:size], n), in_blocks(fresh[:, 0:size], n), factors, ALU.mult).then_inc(scaled_ready, 1)
                    dve.scalar_tensor_tensor(out=part, in0=fresh[:, 0:size], scalar=1.0 / (HOPS + 1), in1=part,
                                             op0=ALU.mult, op1=ALU.add).then_inc(fresh_used, 1)
                else:
                    dve.wait_ge(fresh_used, HOPS * total)
                    dve.wait_ge(scaled_ready, nth)
                    dve.wait_ge(stage_turned, nth + 1)
                    dve.tensor_tensor(in_blocks(fresh[:, 0:size], n), in_blocks(turned[:, 0:size], n),
                                      over_features(inv_third[:, ds(s * FIVE, FIVE)], n), ALU.mult).then_inc(turned_used, 1)
                    dve.wait_ge(turned_used, nth + 1)
                    dve.wait_ge(scaled_stored, nth * 16)
                    dve.tensor_tensor(scaled[:, 0:size], fresh[:, 0:size], part, ALU.add).then_inc(scaled_ready, 1)

            def outside(k):
                dve.wait_ge(added[SLOTS - 1], (k + 1) * turns)
                with dve.Fori(0, groups) as g:
                    steps = g * (blocks + 1) + k * groups * (blocks + 1)
                    dve.wait_ge(rest_hot, g * blocks + k * rest_turns)
                    dve.wait_ge(rest_step, steps)
                    dve.tensor_copy(window[:, :], rest[:, ds(g * CHUNKS, CHUNKS)]).then_inc(rest_step, 1)
                    with dve.Fori(0, blocks) as w:
                        dve.wait_ge(rest_step, steps + w + 1)
                        dve.wait_ge(rest_summed, g * blocks + w + k * rest_turns)
                        dve.tensor_tensor(hot[:, 0, :, :], counting(P), over_hot(window[:, :], P),
                                          ALU.is_equal).then_inc(rest_hot, 1)
                        dve.wait_ge(rest_hot, g * blocks + w + (k * rest_turns + 1))
                        dve.tensor_scalar(window[:, :], window[:, :], float(P), None, ALU.subtract).then_inc(rest_step, 1)
                        dve.wait_ge(rest_added, g * blocks + w + k * rest_turns)
                        dve.wait_ge(rest_summed, g * blocks + w + (k * rest_turns + 1))
                        into = acc[:, ds(w * P, P)]
                        dve.tensor_tensor(into, sums_bank[:, 0, 0:P], into, ALU.add).then_inc(rest_added, 1)
                dve.wait_ge(rest_added, (k + 1) * rest_turns)

            for k in range(1 + HOPS):
                dve.wait_ge(acc_cleared, k * total)
                one_pass(dve, k, turn, own_step, finish, outside)


_INS = ["x", "src", "dst", "edge_type_2", "L0_gnn_W_data", "L0_gnn_b_data", "L0_gnn_W_control",
        "L0_gnn_b_control", "L0_gnn_W_self", "L0_gnn_b_self"]


def kernel(**inputs):
    import numpy as _np
    import concourse.bacc as _bacc
    from concourse.bass_utils import run_bass_kernel_spmd as _run

    nc = _bacc.Bacc("TRN2", target_bir_lowering=False, num_devices=1)
    arrays, args = {}, []
    for name in _INS:
        a = _np.ascontiguousarray(inputs[name])
        arrays[f"in_{name}"] = a
        args.append(nc.dram_tensor(f"in_{name}", a.shape, mybir.dt.from_np(a.dtype), kind="ExternalInput").ap())
    out = nc.dram_tensor("out", arrays["in_x"].shape, F32, kind="ExternalOutput").ap()
    gnn_kernel(nc, *args, out)
    r = _run(nc, [arrays], core_ids=[0])
    return r.results[0]["out"]
```
